# Optimizing a Trainium2 kernel written in Bass

```python
import numpy as np
import jax
import jax.numpy as jnp

def _softmax(x, axis=-1):
    return jax.nn.softmax(x, axis=axis)

def _gelu(x):
    return jax.nn.gelu(x, approximate=True)

def _silu(x):
    return jax.nn.silu(x)

def _sigmoid(x):
    return jax.nn.sigmoid(x)

def _layernorm(x, axis=-1, eps=1e-05):
    m = jnp.mean(x, axis=axis, keepdims=True)
    v = jnp.var(x, axis=axis, keepdims=True)
    return (x - m) / jnp.sqrt(v + eps)

def _scatter_add(tgt, idx, src, axis=0):
    return tgt.at[idx].add(src)

def _segment_sum(src, seg, n):
    return jax.ops.segment_sum(src, seg, n)
kernel_name = 'mk_flamingo_gated_d2_seqx_r8_1e1eac'

def setup_inputs(seed: int=0):
    np.random.seed(seed)
    _w = jnp.asarray

    def _rec_inputs():
        import jax
        import jax.numpy as jnp
        _rk = jax.random.key(seed)
        x = 0.0001212 + 1 * jax.random.normal(jax.random.fold_in(_rk, 1), (16, 128, 256), jnp.float32)
        _lenS = 128 - jax.random.randint(jax.random.fold_in(_rk, 7), (16,), 0, max(1, 128 // 4) + 1, jnp.int32)
        _lenS2 = 128 - jax.random.randint(jax.random.fold_in(_rk, 8), (16,), 0, max(1, 128 // 4) + 1, jnp.int32)
        _ctx_2048P = jax.random.normal(jax.random.fold_in(_rk, 11), (16, 16, 256), jnp.float32)
        _ctx_2048c = jax.random.dirichlet(jax.random.fold_in(_rk, 511), 0.3 * jnp.ones((16,), jnp.float32), (16, 128))
        _ctx_2048t = jnp.einsum('bsk,bkd->bsd', _ctx_2048c, _ctx_2048P)
        _ctx_2048t = _ctx_2048t * jax.lax.rsqrt(jnp.mean(jnp.square(_ctx_2048t)) + 1e-12) * 0.953939
        ctx_2048 = 0.000173663 + 1.0001 * (_ctx_2048t + 0.3 * jax.random.normal(jax.random.fold_in(_rk, 611), (16, 128, 256), jnp.float32))
        _validS = jnp.arange(128)[None, :] < _lenS[:, None]
        _validS2 = jnp.arange(128)[None, :] < _lenS2[:, None]
        _causal = jnp.tril(jnp.ones((128, 128), dtype=bool))
        mask_BxSx4224_bf0 = jnp.logical_not(jnp.ones((16, 128, 528), dtype=bool))
        _g = jax.random.normal(jax.random.fold_in(_rk, 9001), (2, 2), jnp.float32)
        _g = jnp.sign(_g) * jnp.maximum(jnp.abs(_g), 1.0) + (_g == 0) * 1.0
        g_xattn = _g[0]
        g_ffn = _g[1]
        return (x, ctx_2048, mask_BxSx4224_bf0, g_xattn, g_ffn)
    x, ctx_2048, mask_BxSx4224_bf0, g_xattn, g_ffn = _rec_inputs()

    def _L0_xattn_setup():
        import jax, jax.numpy as jnp
        import numpy as np
        B_DIM, T_DIM, C_DIM = (16, 128, 256)

        def _wkv(w, u, k, v):
            Bn, Tn, Cn = k.shape
            NEG_INF = jnp.float32(-1e+38)

            def step(carry, kv_t):
                p, q, o = carry
                kt, vt = kv_t
                no = jnp.maximum(o, u + kt)
                A = jnp.exp(o - no)
                E = jnp.exp(u + kt - no)
                y = (A * p + E * vt) / (A * q + E)
                no2 = jnp.maximum(w + o, kt)
                A2 = jnp.exp(w + o - no2)
                E2 = jnp.exp(kt - no2)
                return ((A2 * p + E2 * vt, A2 * q + E2, no2), y)
            init = (jnp.zeros((Bn, Cn), k.dtype), jnp.zeros((Bn, Cn), k.dtype), jnp.full((Bn, Cn), NEG_INF, k.dtype))
            kT = jnp.moveaxis(k, 1, 0)
            vT = jnp.moveaxis(v, 1, 0)
            _, yT = jax.lax.scan(step, init, (kT, vT))
            return jnp.moveaxis(yT, 0, 1)
        key = jax.random.key(seed)
        k1, k2, k3, k4 = jax.random.split(key, 4)
        w = -jnp.exp(jax.random.normal(k1, (C_DIM,), jnp.float32))
        u = jax.random.normal(k2, (C_DIM,), jnp.float32)
        k = jax.random.normal(k3, (B_DIM, T_DIM, C_DIM), jnp.float32)
        v = jax.random.normal(k4, (B_DIM, T_DIM, C_DIM), jnp.float32)
        return {'B': B_DIM, 'T': T_DIM, 'C': C_DIM, 'w': w, 'u': u, 'k': k, 'v': v}
    _L0_xattn_all = _L0_xattn_setup()
    _L0_xattn_in = {k: v for k, v in _L0_xattn_all.items() if k in ('w', 'u')}
    del _L0_xattn_all

    def _L0_ffn_setup():
        import jax, jax.numpy as jnp
        import numpy as np

        @jax.custom_vjp
        def ste_sign(x):
            return jnp.sign(x)

        def _ste_fwd(x):
            return (jnp.sign(x), None)

        def _ste_bwd(_, g):
            return (g,)
        ste_sign.defvjp(_ste_fwd, _ste_bwd)
        D_MODEL = 256
        D_HIDDEN = 1024
        key = jax.random.key(seed)
        k_x, k_up, k_dn = jax.random.split(key, 3)
        x = jax.random.normal(k_x, (2, 256, D_MODEL), dtype=jnp.float32)
        up_weight = jax.random.normal(k_up, (D_HIDDEN, D_MODEL), dtype=jnp.float32) * 0.02
        down_weight = jax.random.normal(k_dn, (D_MODEL, D_HIDDEN), dtype=jnp.float32) * 0.02
        up_scale = jnp.ones((D_HIDDEN,), dtype=jnp.float32)
        down_scale = jnp.ones((D_MODEL,), dtype=jnp.float32)
        output_scale = jnp.ones((1,), dtype=jnp.float32)
        return {'x': x, 'up_weight': up_weight, 'down_weight': down_weight, 'up_scale': up_scale, 'down_scale': down_scale, 'output_scale': output_scale}
    _L0_ffn_all = _L0_ffn_setup()
    _L0_ffn_in = {k: v for k, v in _L0_ffn_all.items() if k in ('up_weight', 'down_weight', 'up_scale', 'down_scale', 'output_scale')}
    del _L0_ffn_all

    def _L1_xattn_setup():
        import jax, jax.numpy as jnp
        import numpy as np
        import math
        DIM = 256
        B, Q_LEN, KV_LEN = (8, 128, 512)
        key = jax.random.key(seed)
        ks = jax.random.split(key, 8)
        x = jax.random.normal(ks[0], (B, Q_LEN, DIM), dtype=jnp.float32)
        mask = jnp.zeros((B, Q_LEN, KV_LEN + Q_LEN), dtype=bool)
        k_cache = jax.random.normal(ks[1], (B, KV_LEN, DIM), dtype=jnp.float32)
        v_cache = jax.random.normal(ks[2], (B, KV_LEN, DIM), dtype=jnp.float32)
        scale = 1.0 / math.sqrt(DIM)
        wq = jax.random.normal(ks[3], (DIM, DIM), dtype=jnp.float32) * scale
        wk = jax.random.normal(ks[4], (DIM, DIM), dtype=jnp.float32) * scale
        wv = jax.random.normal(ks[5], (DIM, DIM), dtype=jnp.float32) * scale
        wo = jax.random.normal(ks[6], (DIM, DIM), dtype=jnp.float32) * scale
        return {'x': x, 'mask': mask, 'k_cache': k_cache, 'v_cache': v_cache, 'wq': wq, 'wk': wk, 'wv': wv, 'wo': wo}
    _L1_xattn_all = _L1_xattn_setup()
    _L1_xattn_in = {k: v for k, v in _L1_xattn_all.items() if k in ('wq', 'wk', 'wv', 'wo')}
    del _L1_xattn_all

    def _L1_ffn_setup():
        import jax, jax.numpy as jnp
        import numpy as np
        NUM_ROUTED = 7
        TOP_K = 3
        D = 256
        H = 256
        B, S = (4, 256)

        def _expert_ffn(x, w1, wg, w2):
            return jax.nn.silu(x @ w1) * (x @ wg) @ w2
        key = jax.random.key(seed)
        ks = jax.random.split(key, 8)
        s = 0.02
        return {'x': jax.random.normal(ks[0], (B, S, D), jnp.float32), 'W1': jax.random.normal(ks[1], (NUM_ROUTED, D, H), jnp.float32) * s, 'Wg': jax.random.normal(ks[2], (NUM_ROUTED, D, H), jnp.float32) * s, 'W2': jax.random.normal(ks[3], (NUM_ROUTED, H, D), jnp.float32) * s, 'Ws1': jax.random.normal(ks[4], (D, H), jnp.float32) * s, 'Wsg': jax.random.normal(ks[5], (D, H), jnp.float32) * s, 'Ws2': jax.random.normal(ks[6], (H, D), jnp.float32) * s, 'gate_w': jax.random.normal(ks[7], (D, NUM_ROUTED), jnp.float32) * s, 'gate_b': jnp.zeros((NUM_ROUTED,), jnp.float32), 'biases': jnp.zeros((NUM_ROUTED,), jnp.float32)}
    _L1_ffn_all = _L1_ffn_setup()
    _L1_ffn_in = {k: v for k, v in _L1_ffn_all.items() if k in ('W1', 'Wg', 'W2', 'Ws1', 'Wsg', 'Ws2', 'gate_w', 'gate_b', 'biases')}
    del _L1_ffn_all
    return {'x': x, 'ctx_2048': ctx_2048, 'mask_BxSx4224_bf0': mask_BxSx4224_bf0, 'g_xattn': g_xattn, 'g_ffn': g_ffn, 'L0_xattn_w': _L0_xattn_in['w'], 'L0_xattn_u': _L0_xattn_in['u'], 'L0_ffn_up_weight': _L0_ffn_in['up_weight'], 'L0_ffn_down_weight': _L0_ffn_in['down_weight'], 'L0_ffn_up_scale': _L0_ffn_in['up_scale'], 'L0_ffn_down_scale': _L0_ffn_in['down_scale'], 'L0_ffn_output_scale': _L0_ffn_in['output_scale'], 'L1_xattn_wq': _L1_xattn_in['wq'], 'L1_xattn_wk': _L1_xattn_in['wk'], 'L1_xattn_wv': _L1_xattn_in['wv'], 'L1_xattn_wo': _L1_xattn_in['wo'], 'L1_ffn_W1': _L1_ffn_in['W1'], 'L1_ffn_Wg': _L1_ffn_in['Wg'], 'L1_ffn_W2': _L1_ffn_in['W2'], 'L1_ffn_Ws1': _L1_ffn_in['Ws1'], 'L1_ffn_Wsg': _L1_ffn_in['Wsg'], 'L1_ffn_Ws2': _L1_ffn_in['Ws2'], 'L1_ffn_gate_w': _L1_ffn_in['gate_w'], 'L1_ffn_gate_b': _L1_ffn_in['gate_b'], 'L1_ffn_biases': _L1_ffn_in['biases']}

def reference(x, ctx_2048, mask_BxSx4224_bf0, g_xattn, g_ffn, L0_xattn_w, L0_xattn_u, L0_ffn_up_weight, L0_ffn_down_weight, L0_ffn_up_scale, L0_ffn_down_scale, L0_ffn_output_scale, L1_xattn_wq, L1_xattn_wk, L1_xattn_wv, L1_xattn_wo, L1_ffn_W1, L1_ffn_Wg, L1_ffn_W2, L1_ffn_Ws1, L1_ffn_Wsg, L1_ffn_Ws2, L1_ffn_gate_w, L1_ffn_gate_b, L1_ffn_biases):
    import jax
    import jax.numpy as jnp

    def _L0_xattn_ref(B, T, C, w, u, k, v):
        import jax, jax.numpy as jnp
        import numpy as np
        B_DIM, T_DIM, C_DIM = (16, 128, 256)

        def _wkv(w, u, k, v):
            Bn, Tn, Cn = k.shape
            NEG_INF = jnp.float32(-1e+38)

            def step(carry, kv_t):
                p, q, o = carry
                kt, vt = kv_t
                no = jnp.maximum(o, u + kt)
                A = jnp.exp(o - no)
                E = jnp.exp(u + kt - no)
                y = (A * p + E * vt) / (A * q + E)
                no2 = jnp.maximum(w + o, kt)
                A2 = jnp.exp(w + o - no2)
                E2 = jnp.exp(kt - no2)
                return ((A2 * p + E2 * vt, A2 * q + E2, no2), y)
            init = (jnp.zeros((Bn, Cn), k.dtype), jnp.zeros((Bn, Cn), k.dtype), jnp.full((Bn, Cn), NEG_INF, k.dtype))
            kT = jnp.moveaxis(k, 1, 0)
            vT = jnp.moveaxis(v, 1, 0)
            _, yT = jax.lax.scan(step, init, (kT, vT))
            return jnp.moveaxis(yT, 0, 1)
        return _wkv(w, u, k, v)

    def _L0_ffn_ref(x, up_weight, down_weight, up_scale, down_scale, output_scale):
        import jax, jax.numpy as jnp
        import numpy as np

        @jax.custom_vjp
        def ste_sign(x):
            return jnp.sign(x)

        def _ste_fwd(x):
            return (jnp.sign(x), None)

        def _ste_bwd(_, g):
            return (g,)
        ste_sign.defvjp(_ste_fwd, _ste_bwd)
        D_MODEL = 256
        D_HIDDEN = 1024
        up_w = ste_sign(up_weight)
        down_w = ste_sign(down_weight)
        hidden = jnp.einsum('bsd,hd->bsh', x, up_w) * up_scale
        hidden = jax.nn.relu(hidden)
        out = jnp.einsum('bsh,dh->bsd', hidden, down_w) * down_scale
        return out * output_scale

    def _L1_xattn_ref(x, mask, k_cache, v_cache, wq, wk, wv, wo):
        import jax, jax.numpy as jnp
        import numpy as np
        import math
        DIM = 256
        B, Q_LEN, KV_LEN = (8, 128, 512)
        q = jnp.einsum('bsd,ed->bse', x, wq)
        k_new = jnp.einsum('bsd,ed->bse', x, wk)
        v_new = jnp.einsum('bsd,ed->bse', x, wv)
        k = jnp.concatenate([k_cache, k_new], axis=1)
        v = jnp.concatenate([v_cache, v_new], axis=1)
        scale = 1.0 / math.sqrt(q.shape[-1])
        scores = jnp.einsum('bqd,bkd->bqk', q, k) * scale
        attn = jax.nn.softmax(scores, axis=-1)
        out = jnp.einsum('bqk,bkd->bqd', attn, v)
        return jnp.einsum('bqd,ed->bqe', out, wo)

    def _L1_ffn_ref(x, W1, Wg, W2, Ws1, Wsg, Ws2, gate_w, gate_b, biases):
        import jax, jax.numpy as jnp
        import numpy as np
        NUM_ROUTED = 7
        TOP_K = 3
        D = 256
        H = 256
        B, S = (4, 256)

        def _expert_ffn(x, w1, wg, w2):
            return jax.nn.silu(x @ w1) * (x @ wg) @ w2
        output = _expert_ffn(x, Ws1, Wsg, Ws2)
        gate_logits = x @ gate_w + gate_b
        gate_probas = jax.nn.softmax(gate_logits, axis=-1)
        biased_probas = gate_probas + biases
        _, topk_idxs = jax.lax.top_k(biased_probas, TOP_K)
        topk_probas = jnp.take_along_axis(gate_probas, topk_idxs, axis=-1)
        topk_probas = topk_probas / jnp.sum(topk_probas, axis=-1, keepdims=True)
        for e in range(NUM_ROUTED):
            w_e = jnp.sum(topk_probas * (topk_idxs == e), axis=-1)
            output = output + _expert_ffn(x, W1[e], Wg[e], W2[e]) * w_e[..., None]
        return output
    x = x + jnp.tanh(g_xattn[0]) * _L0_xattn_ref(16, 128, 256, L0_xattn_w, L0_xattn_u, _layernorm(x, axis=-1), ctx_2048)
    x = x + jnp.tanh(g_ffn[0]) * _L0_ffn_ref(_layernorm(x, axis=-1), L0_ffn_up_weight, L0_ffn_down_weight, L0_ffn_up_scale, L0_ffn_down_scale, L0_ffn_output_scale)
    x = x + jnp.tanh(g_xattn[1]) * _L1_xattn_ref(_layernorm(x, axis=-1), mask_BxSx4224_bf0, ctx_2048, ctx_2048, L1_xattn_wq, L1_xattn_wk, L1_xattn_wv, L1_xattn_wo)
    x = x + jnp.tanh(g_ffn[1]) * _L1_ffn_ref(_layernorm(x, axis=-1), L1_ffn_W1, L1_ffn_Wg, L1_ffn_W2, L1_ffn_Ws1, L1_ffn_Wsg, L1_ffn_Ws2, L1_ffn_gate_w, L1_ffn_gate_b, L1_ffn_biases)
    return x

_drawn_inputs = setup_inputs


def setup_inputs(seed=0):
    import zlib

    import numpy as np

    out = dict(_drawn_inputs(seed))
    spreads = {'g_ffn': (-1.0, 0.6),
     'L0_ffn_up_scale': (1.0, 0.2),
     'L0_ffn_down_scale': (1.0, 0.2),
     'L1_ffn_gate_b': (0.0, 2.0),
     'L1_ffn_biases': (0.0, 2.0)}
    factors = {'L1_xattn_wq': 8.0,
     'L1_xattn_wk': 8.0,
     'L1_xattn_wv': 8.0,
     'L1_xattn_wo': 8.0,
     'L1_ffn_W1': 8.0,
     'L1_ffn_Wg': 8.0,
     'L1_ffn_W2': 8.0,
     'L1_ffn_Ws1': 8.0,
     'L1_ffn_Wsg': 8.0,
     'L1_ffn_Ws2': 8.0,
     'L1_ffn_gate_w': 21.674}
    for name, (base, spread) in spreads.items():
        noise = np.random.default_rng([zlib.crc32(name.encode()), seed]).standard_normal(out[name].shape)
        drawn = base * np.exp(spread * noise) if base else spread * noise
        out[name] = jnp.asarray(drawn.astype(out[name].dtype))
    for name, factor in factors.items():
        out[name] = (out[name] * factor).astype(out[name].dtype)
    return out
```

```python
import concourse.bass as bass
from concourse import mybir
from contextlib import ExitStack

F32 = mybir.dt.float32
F32R = mybir.dt.float32r
ALU = mybir.AluOpType
ACT = mybir.ActivationFunctionType
AX_X = mybir.AxisListType.X

P = 128
EPS = 1e-5
NEVER = -1e30
TOP_K = 3
SLOTS = 25
RING = 3
ROUTER_STEPS = 16

KTR, YTR = 3, 13
LTR1, UP, DN = 1, (2, 3, 4, 5), (4, 5, 6, 7)
LTR2, QKV_Q, QKV_K, QKV_V = 9, 11, 11, 12
SCORE, PTR, PV, OTR, WO, LTR3 = 14, 16, 18, 19, 21, 23
GATE = 1


def flamingo_kernel(nc, x, ctx_in, ctxT_in, g_xattn, g_ffn, w_in, w_cols, u_cols, upT_in, downT_in, up_cols,
                    down_scale, output_scale, wqT_in, wkT_in, wvT_in, woT_in, W1, Wg, W2, Ws1, Wsg,
                    Ws2, gate_w, gate_b, biases, out):
    B, T, D = x.shape
    C = D // P
    H = upT_in.shape[1]
    M = H // P
    NE = W1.shape[0] + 1
    NR = W1.shape[0]
    G = 2
    NG = B // G
    N = G * T
    PAIRS = M // 2
    assert T == P and C == 2 and NE == 8 and N * 2 == 512

    ctx = ExitStack()
    with ctx:
        def sb(name, shape, dt=F32):
            return ctx.enter_context(nc.sbuf_tensor(name, shape, dt))

        def bank(name):
            return ctx.enter_context(nc.psum_tensor(name, [P, 512], F32))

        bank_h1 = [bank("h1_0"), bank("h1_1")]
        bank_h2 = [bank("h2_0"), bank("h2_1")]
        bank_out = bank("expert_out")
        side = [bank(f"side{i}") for i in range(3)]

        moe_hi = sb("moe_hi", [P, NE, 3, C, D], F32R)
        moe_lo = sb("moe_lo", [P, NE, 3, C, D], F32R)
        up_sign = sb("up_sign", [P, C, H], F32R)
        down_sign = sb("down_sign", [P, M, D], F32R)
        att_hi = sb("att_hi", [P, 4, C, D], F32R)
        att_lo = sb("att_lo", [P, 4, C, D], F32R)
        gate_raw = sb("gate_raw", [P, C, NE])
        gate_hi = sb("gate_hi", [P, C, NE], F32R)
        gate_lo = sb("gate_lo", [P, C, NE], F32R)

        ident = sb("ident", [P, P])
        wu = sb("wu", [P, 2, C])
        chan = sb("chan", [P, 6, C])
        decay = sb("decay", [P, C, G, T])
        ramp = sb("ramp", [P, D])
        time_col = sb("time_col", [P, 1])
        gates_raw = sb("gates_raw", [P, 5])
        gates = sb("gates", [P, 4])
        half_gate = sb("half_gate", [P, 1])
        down_row = sb("down_row", [P, D])
        up_col = sb("up_col", [P, M])
        router_bias = sb("router_bias", [P, 2, NE])
        earlier = sb("earlier", [P, NE, NE])
        minus_half = sb("minus_half", [P, G])
        eps = sb("eps", [P, G])

        xw = sb("xw", [P, G, D])
        vT = sb("vT", [P, C, G, T])
        ea = sb("ea", [P, C, G, T])
        eb = sb("eb", [P, C, G, T])
        p_state = sb("p_state", [P, 1 + C * N])
        q_state = sb("q_state", [P, 1 + C * N])
        p_late, q_late = p_state[:, 0:C * N], q_state[:, 0:C * N]
        xwn = p_late.rearrange("p (b d) -> p b d", b=G)
        stat_w = sb("stat_w", [P, G, 6])
        mv_w = sb("mv_w", [P, G, 2])
        rstd_w = sb("rstd_w", [P, 2, G])
        x1 = sb("x1", [P, G, D])
        stat_1 = sb("stat_1", [P, G, 6])
        mv_1 = sb("mv_1", [P, G, 2])
        rstd_1 = sb("rstd_1", [P, 2, G])
        x23 = sb("x23", [P, G, D])
        xfn = sb("xfn", [P, G, D])
        att = xfn
        stat_f = sb("stat_f", [P, G, 6])
        mv_f = sb("mv_f", [P, G, 2])
        rstd_f = sb("rstd_f", [P, 2, G])
        xh = sb("xh", [P, C, N], F32R)
        xl = sb("xl", [P, C, N], F32R)
        pth = xh[:].rearrange("p k (b t) -> p k b t", b=G)
        ptl = xl[:].rearrange("p k (b t) -> p k b t", b=G)
        hid = sb("hid", [P, 2 * N])
        prob = hid[:].rearrange("p (b k t) -> p b k t", b=G, k=2)
        hid_hi = sb("hid_hi", [P, 2, 2, N], F32R)
        hid_lo = sb("hid_lo", [P, 2, 2, N], F32R)
        qh, ql = hid_hi[:, 0], hid_lo[:, 0]
        oh, ol = hid_hi[:, 1], hid_lo[:, 1]
        ctxT_a = sb("ctxT_a", [P, C, G, T])
        ctx_a = sb("ctx_a", [P, G, D])
        kh = sb("kh", [P, 2, C, G, T], F32R)
        kl = sb("kl", [P, 2, C, G, T], F32R)
        vh = sb("vh", [P, 2, G, D], F32R)
        vl = sb("vl", [P, 2, G, D], F32R)
        row_max = sb("row_max", [P, 2, G])
        row_sum = sb("row_sum", [P, G])
        row_inv = sb("row_inv", [P, G])
        xmh = sb("xmh", [P, C, N], F32R)
        xml = sb("xml", [P, C, N], F32R)
        work = sb("work", [P, 3, C * N])
        act_buf = work[:, 0:2]
        acc = work[:, 2].rearrange("p (b d) -> p b d", b=G)
        gated_hi = sb("gated_hi", [P, 2, C, N], F32R)
        gated_lo = sb("gated_lo", [P, 2, C, N], F32R)
        prb = sb("prb", [P, 6, G, NE])
        cmp_gt = sb("cmp_gt", [P, G, NE, NE])
        cmp_eq = sb("cmp_eq", [P, G, NE, NE])
        red = sb("red", [P, 5, G])
        wgt = sb("wgt", [P, G, NE])

        pieces = [upT_in.rearrange("(c p) h -> p c h", p=P)[:, :, j * D:(j + 1) * D] for j in range(H // D)]
        pieces += [downT_in.rearrange("(m p) d -> p m d", p=P)[:, 2 * j:2 * j + 2, :] for j in range(M // 2)]
        SIGNS = len(pieces)
        signs = [up_sign[:, :, j * D:(j + 1) * D] for j in range(H // D)]
        signs += [down_sign[:, 2 * j:2 * j + 2, :] for j in range(M // 2)]
        pieces += [w.rearrange("(c p) n -> p c n", p=P) for w in (wqT_in, wkT_in, wvT_in, woT_in)]
        splits = [(att_hi[:, i], att_lo[:, i]) for i in range(4)]
        LAYER_PIECES = len(pieces)
        for e in range(NE):
            for i, w in enumerate((W1[e], Wg[e], W2[e]) if e < NR else (Ws1, Wsg, Ws2)):
                pieces.append(w.rearrange("(c p) n -> p c n", p=P))
                splits.append((moe_hi[:, e, i], moe_lo[:, e, i]))

        names = """
        ld_x ld_v ld_ctxT ld_ctx ld_wu ld_ramp ld_gates ld_upcol ld_drow ld_gatew ld_rbias
        ld_piece0 ld_piece1 ld_piece2 stored
        ident_ready consts_pool bias_fill chan_step decay_step ramp_ready gates_ready scales_ready
        gate_hi_ready gate_lo_ready sign_neg sign_done split_hi_done split_lo_done
        w_stat w_mv w_rv w_rstd w_norm w_ramped ktr_done exp_done q_scanned den_ready den_inv
        eav_ready p_scanned ebv_ready num_ready y_raw y_ready ytr_done x1_ready
        stat1_step mv1_step rv1_step rstd1_ready f_stat f_mv f_rv f_rstd xn_ready
        ltr1_done ltr2_done ltr3_done xh_ready xl_ready up_done hid_ready hid_hi_ready hid_lo_ready
        dn_done ffn_scaled x2_ready kc_hi kc_lo vc_hi vc_lo q_done k_done v_done qh_ready ql_ready kh_ready
        kl_ready vh_ready vl_ready score_done max_ready negmax_ready exp_p_done rowinv_ready ptr_done
        pth_ready ptl_ready pv_done att_scaled otr_done oh_ready ol_ready wo_done x3_ready
        xmh_ready xml_ready
        h1_done tanh_done act_done h2_done gated_ready ghi_ready glo_ready out_done acc_done
        logits_done r_step r_centred r_exp wgt_ready
        """.split()
        s = {n: ctx.enter_context(nc.semaphore(n)) for n in names}

        def wait(eng, sem, value):
            if not (isinstance(value, int) and value <= 0):
                eng.wait_ge(sem, value)

        x_g = x.rearrange("(g b) t d -> t (g b) d", b=G)
        out_g = out.rearrange("(g b) t d -> t (g b) d", b=G)
        ctx_g = ctx_in.rearrange("(g b) t d -> t (g b) d", b=G)
        ctxT_g = ctxT_in.rearrange("(g b) (c p) t -> p c (g b) t", b=G, p=P)

        def group(g):
            return bass.ds(g * G, G)

        def f32(ap):
            return ap.bitcast(F32)

        def flat(ap):
            return ap.rearrange("p a b -> p (a b)")

        def flat3(ap):
            return ap.rearrange("p a b c -> p (a b c)")

        landed = (s["ld_piece0"], s["ld_piece1"], s["ld_piece2"])

        def piece_of(layer, slot):
            if layer:
                return LAYER_PIECES + slot
            return slot - 1 if 1 <= slot <= LAYER_PIECES else len(pieces)

        block = ctx.enter_context(nc.Block())

        @block.sync
        def _(sp):
            def load_wkv(g):
                for c in range(C):
                    sp.dma_start(vT[:, c], ctxT_g[:, c, group(g), :]).then_inc(s["ld_v"], 16)
                sp.dma_start(xw[:], x_g[:, group(g), :]).then_inc(s["ld_x"], 16)

            def load_ctx(g):
                for c in range(C):
                    sp.dma_start(ctxT_a[:, c], ctxT_g[:, c, group(g), :]).then_inc(s["ld_ctxT"], 16)
                sp.dma_start(ctx_a[:], ctx_g[:, group(g), :]).then_inc(s["ld_ctx"], 16)

            def next_ctx(f):
                sp.wait_ge(s["kc_lo"], f + 1)
                sp.wait_ge(s["vc_lo"], f + 1)
                load_ctx(f + 1)

            def next_wkv(g):
                sp.wait_ge(s["x1_ready"], g + 1)
                load_wkv(g + 1)

            def store(g):
                sp.wait_ge(s["acc_done"], NE * g + NE)
                sp.dma_start(out_g[:, group(g), :], acc[:]).then_inc(s["stored"], 16)

            def load_piece(n):
                if n >= RING:
                    if n - RING < SIGNS:
                        sp.wait_ge(s["sign_done"], n - RING + 1)
                    else:
                        sp.wait_ge(s["split_lo_done"], n - RING - SIGNS + 1)
                sp.dma_start(work[:, n % RING].rearrange("p (c n) -> p c n", c=2), pieces[n]).then_inc(landed[n % RING], 16)

            sp.dma_start(xw[:], x_g[:, group(0), :]).then_inc(s["ld_x"], 16)
            sp.dma_start(wu[:, 0], w_cols).then_inc(s["ld_wu"], 16)
            sp.dma_start(wu[:, 1], u_cols).then_inc(s["ld_wu"], 16)
            sp.dma_start(ramp[:], w_in.rearrange("(a d) -> a d", a=1).to_broadcast([P, D])).then_inc(s["ld_ramp"], 16)
            for c in range(C):
                sp.dma_start(vT[:, c], ctxT_g[:, c, group(0), :]).then_inc(s["ld_v"], 16)
            for n in range(RING):
                load_piece(n)
            for i, g in enumerate((g_xattn, g_ffn)):
                sp.dma_start(gates_raw[:, 2 * i:2 * i + 2],
                             g.rearrange("(a d) -> a d", a=1).to_broadcast([P, 2])).then_inc(s["ld_gates"], 16)
            sp.dma_start(gates_raw[:, 4:5],
                         output_scale.rearrange("(a d) -> a d", a=1).to_broadcast([P, 1])).then_inc(s["ld_gates"], 16)
            sp.dma_start(down_row[:], down_scale.rearrange("(a d) -> a d", a=1).to_broadcast([P, D])).then_inc(s["ld_drow"], 16)
            sp.dma_start(up_col[:], up_cols).then_inc(s["ld_upcol"], 16)
            load_ctx(0)
            sp.wait_ge(s["bias_fill"], 2)
            for i, r in enumerate((gate_b, biases)):
                sp.dma_start(router_bias[:, i, 0:NR],
                             r.rearrange("(a d) -> a d", a=1).to_broadcast([P, NR])).then_inc(s["ld_rbias"], 16)
            sp.dma_start(gate_raw[:, :, 0:NR], gate_w.rearrange("(c p) e -> p c e", p=P)).then_inc(s["ld_gatew"], 16)
            for n in range(RING, LAYER_PIECES):
                load_piece(n)
            next_wkv(0)
            for n in range(LAYER_PIECES, len(pieces)):
                load_piece(n)
            next_ctx(0)
            next_wkv(1)
            with sp.Fori(0, NG - 3) as g:
                next_ctx(g + 1)
                next_wkv(g + 2)
                store(g)
            next_ctx(NG - 2)
            for g in range(NG - 3, NG):
                store(g)
            sp.wait_ge(s["stored"], 16 * NG)

        @block.tensor
        def _(pe):
            def transpose8(dst, src):
                for c in range(C):
                    for b in range(G):
                        last = nc.tensor.transpose(dst[:, (c * G + b) * P:(c * G + b + 1) * P],
                                                   src[:, b, c * P:(c + 1) * P], ident[:])
                return last

            def three_pass(dst, pairs):
                steps = [ops for (ah, al), (bh, bl) in pairs for ops in ((ah, bh), (al, bh), (ah, bl))]
                for i, (a, b) in enumerate(steps):
                    last = nc.tensor.matmul(dst, a, b, start=(i == 0), stop=(i == len(steps) - 1))
                return last

            def weights_by_tokens(dst, hi, lo, col0, mh, ml):
                for n in range(2):
                    cols = slice(col0 + n * P, col0 + (n + 1) * P)
                    last = three_pass(dst[:, n * N:(n + 1) * N],
                                      [((hi[:, d, cols], lo[:, d, cols]), (mh[:, d], ml[:, d])) for d in range(C)])
                return last

            def tokens_by_weights(dst, mh, ml, hi, lo):
                for b in range(G):
                    tok = slice(b * P, (b + 1) * P)
                    last = three_pass(dst[:, b * D:(b + 1) * D],
                                      [((mh[:, d, tok], ml[:, d, tok]), (hi[:, d], lo[:, d])) for d in range(C)])
                return last

            def expert_slot(g, slot):
                e, part = divmod(slot, 3)
                if slot < 3 * NE and part == 0:
                    if e == 0:
                        pe.wait_ge(s["xmh_ready"], g + 1)
                        pe.wait_ge(s["xml_ready"], g + 1)
                    wait(pe, s["act_done"], NE * g + max(e - 1, 0))
                    weights_by_tokens(bank_h1[e % 2], moe_hi[:, e, 0], moe_lo[:, e, 0], 0, xmh, xml).then_inc(s["h1_done"], 1)
                elif slot < 3 * NE and part == 1:
                    wait(pe, s["gated_ready"], NE * g + max(e - 1, 0))
                    weights_by_tokens(bank_h2[e % 2], moe_hi[:, e, 1], moe_lo[:, e, 1], 0, xmh, xml).then_inc(s["h2_done"], 1)
                    if slot == GATE:
                        wait(pe, s["acc_done"], NE * g)
                        for b in range(G):
                            tok = slice(b * P, (b + 1) * P)
                            last = three_pass(bank_out[:, b * NE:(b + 1) * NE],
                                              [((xmh[:, d, tok], xml[:, d, tok]), (gate_hi[:, d], gate_lo[:, d]))
                                               for d in range(C)])
                        last.then_inc(s["logits_done"], 1)
                else:
                    d = e - 1
                    if d < 0:
                        return
                    pe.wait_ge(s["glo_ready"], NE * g + d + 1)
                    if d == 0:
                        pe.wait_ge(s["r_step"], ROUTER_STEPS * g + 1)
                    else:
                        pe.wait_ge(s["acc_done"], NE * g + d)
                    tokens_by_weights(bank_out, gated_hi[:, d % 2], gated_lo[:, d % 2],
                                      moe_hi[:, d, 2], moe_lo[:, d, 2]).then_inc(s["out_done"], 1)

            def wkv_slot(g, slot):
                if slot == KTR:
                    pe.wait_ge(s["w_ramped"], g + 1)
                    wait(pe, s["xh_ready"], 2 * g - 1)
                    wait(pe, s["xl_ready"], 2 * g - 1)
                    transpose8(side[0], xwn).then_inc(s["ktr_done"], 1)
                if slot == YTR:
                    pe.wait_ge(s["y_ready"], g + 1)
                    wait(pe, s["kh_ready"], g)
                    wait(pe, s["kl_ready"], g)
                    for b in range(G):
                        for c in range(C):
                            last = nc.tensor.transpose(side[1][:, b * D + c * P:b * D + (c + 1) * P],
                                                       ea[:, c, b], ident[:])
                    last.then_inc(s["ytr_done"], 1)

            def layer_slot(f, slot, beside_wkv):
                if slot == LTR1:
                    pe.wait_ge(s["xn_ready"], 3 * f + 1)
                    wait(pe, s["xmh_ready"], f)
                    wait(pe, s["xml_ready"], f)
                    transpose8(side[0], xfn).then_inc(s["ltr1_done"], 1)
                for p in range(PAIRS):
                    if slot == UP[p]:
                        if p == 0:
                            pe.wait_ge(s["xh_ready"], 2 * f + 1)
                            pe.wait_ge(s["xl_ready"], 2 * f + 1)
                        else:
                            pe.wait_ge(s["hid_ready"], PAIRS * f + p)
                        for k in range(2):
                            m = 2 * p + k
                            for i, (d, part) in enumerate([(d, part) for d in range(C) for part in (xh, xl)]):
                                last = nc.tensor.matmul(side[2][:, k * N:(k + 1) * N], up_sign[:, d, m * P:(m + 1) * P],
                                                        part[:, d], start=(i == 0), stop=(i == 2 * C - 1))
                        last.then_inc(s["up_done"], 1)
                    if slot == DN[p]:
                        pe.wait_ge(s["hid_lo_ready"], PAIRS * f + p + 1)
                        for k in range(2):
                            for b in range(G):
                                for part in (hid_hi, hid_lo):
                                    last = nc.tensor.matmul(
                                        side[1][:, b * D:(b + 1) * D], part[:, p % 2, k, b * P:(b + 1) * P],
                                        down_sign[:, 2 * p + k],
                                        start=(p == 0 and k == 0 and b == 0 and part is hid_hi),
                                        stop=(p == PAIRS - 1 and k == 1 and part is hid_lo), skip_group_check=True)
                        last.then_inc(s["dn_done"], 1)
                if slot == LTR2:
                    pe.wait_ge(s["xn_ready"], 3 * f + 2)
                    if beside_wkv:
                        pe.wait_ge(s["exp_done"], f + 2)
                    transpose8(side[0], xfn).then_inc(s["ltr2_done"], 1)
                if slot == QKV_Q:
                    pe.wait_ge(s["xh_ready"], 2 * f + 2)
                    pe.wait_ge(s["xl_ready"], 2 * f + 2)
                    weights_by_tokens(side[2], att_hi[:, 0], att_lo[:, 0], 0, xh, xl).then_inc(s["q_done"], 1)
                if slot == QKV_K:
                    weights_by_tokens(side[1], att_hi[:, 1], att_lo[:, 1], 0, xh, xl).then_inc(s["k_done"], 1)
                if slot == QKV_V:
                    tokens_by_weights(side[0], xh, xl, att_hi[:, 2], att_lo[:, 2]).then_inc(s["v_done"], 1)
                if slot == SCORE:
                    for ready in (s["qh_ready"], s["ql_ready"], s["kh_ready"], s["kl_ready"], s["kc_lo"]):
                        pe.wait_ge(ready, f + 1)
                    for b in range(G):
                        tok = slice(b * P, (b + 1) * P)
                        last = three_pass(side[2][:, b * 2 * T:(b + 1) * 2 * T],
                                          [((qh[:, c, tok], ql[:, c, tok]), (kh[:, :, c, b], kl[:, :, c, b]))
                                           for c in range(C)])
                    last.then_inc(s["score_done"], 1)
                if slot == PTR:
                    pe.wait_ge(s["exp_p_done"], f + 1)
                    if beside_wkv:
                        pe.wait_ge(s["x1_ready"], f + 2)
                    for part in range(2):
                        for b in range(G):
                            last = nc.tensor.transpose(side[1][:, (part * G + b) * P:(part * G + b + 1) * P],
                                                       prob[:, b, part], ident[:])
                    last.then_inc(s["ptr_done"], 1)
                if slot == PV:
                    for ready in (s["pth_ready"], s["ptl_ready"], s["vh_ready"], s["vl_ready"], s["vc_lo"]):
                        pe.wait_ge(ready, f + 1)
                    for b in range(G):
                        last = three_pass(side[0][:, b * D:(b + 1) * D],
                                          [((pth[:, part, b], ptl[:, part, b]), (vh[:, part, b], vl[:, part, b]))
                                           for part in range(2)])
                    last.then_inc(s["pv_done"], 1)
                if slot == OTR:
                    pe.wait_ge(s["att_scaled"], f + 1)
                    transpose8(side[2], att).then_inc(s["otr_done"], 1)
                if slot == WO:
                    pe.wait_ge(s["oh_ready"], f + 1)
                    pe.wait_ge(s["ol_ready"], f + 1)
                    tokens_by_weights(side[1], oh, ol, att_hi[:, 3], att_lo[:, 3]).then_inc(s["wo_done"], 1)
                if slot == LTR3:
                    pe.wait_ge(s["xn_ready"], 3 * f + 3)
                    transpose8(side[0], xfn).then_inc(s["ltr3_done"], 1)

            def passage(g, experts, layer, wkv):
                for slot in range(SLOTS):
                    if experts:
                        expert_slot(g, slot)
                    if wkv:
                        wkv_slot(g + 2, slot)
                    if layer:
                        layer_slot(g + 1, slot, wkv)

            pe.wait_ge(s["ident_ready"], 2)
            passage(-2, False, False, True)
            pe.wait_ge(s["sign_done"], SIGNS)
            pe.wait_ge(s["split_lo_done"], LAYER_PIECES - SIGNS)
            passage(-1, False, True, True)
            pe.wait_ge(s["gate_lo_ready"], 1)
            pe.wait_ge(s["split_lo_done"], len(splits))
            passage(0, True, True, True)
            with pe.Fori(1, NG - 2) as g:
                passage(g, True, True, True)
            passage(NG - 2, True, True, False)
            passage(NG - 1, True, False, False)

        @block.scalar
        def _(act):
            def expert_slot(g, slot):
                e, part = divmod(slot, 3)
                if slot >= 3 * NE:
                    return
                if part == 0:
                    act.wait_ge(s["h1_done"], NE * g + e + 1)
                    wait(act, s["glo_ready"], NE * g + max(e - 1, 0))
                    nc.scalar.activation(act_buf[:, e % 2], bank_h1[e % 2][:], ACT.Tanh, scale=0.5).then_inc(s["tanh_done"], 1)
                if part == 1:
                    act.wait_ge(s["gated_ready"], NE * g + e + 1)
                    wait(act, s["out_done"], NE * g + max(e - 1, 0))
                    nc.scalar.activation(flat(gated_hi[:, e % 2]), act_buf[:, e % 2], ACT.Copy).then_inc(s["ghi_ready"], 1)
                if slot == 3:
                    act.wait_ge(s["r_centred"], g + 1)
                    nc.scalar.activation(prb[:, 1], prb[:, 0], ACT.Exp).then_inc(s["r_exp"], 1)

            def wkv_slot(g, slot):
                if slot == KTR:
                    act.wait_ge(s["ktr_done"], g + 1)
                    if isinstance(g, int) and g == 0:
                        act.wait_ge(s["chan_step"], 7)
                    for dst, row in ((ea, 3), (eb, 4)):
                        for c in range(C):
                            last = nc.scalar.activation(flat(dst[:, c]), side[0][:, c * N:(c + 1) * N], ACT.Exp,
                                                        bias=chan[:, row, c:c + 1])
                    last.then_inc(s["exp_done"], 1)

            def split_hi(dst, src, done, scale=1.0):
                nc.scalar.activation(dst, src, ACT.Copy, scale=scale).then_inc(done, 1)

            def layer_slot(f, slot):
                if slot == LTR1:
                    act.wait_ge(s["ltr1_done"], f + 1)
                    split_hi(flat(xh[:]), side[0][:], s["xh_ready"])
                if slot == UP[0]:
                    act.wait_ge(s["ld_ctxT"], 16 * C * (f + 1))
                    wait(act, s["score_done"], f)
                    split_hi(flat3(kh[:, 0]), flat3(ctxT_a[:]), s["kc_hi"])
                    act.wait_ge(s["ld_ctx"], 16 * (f + 1))
                    wait(act, s["pv_done"], f)
                    split_hi(flat(vh[:, 0]), flat(ctx_a[:]), s["vc_hi"])
                for p in range(PAIRS):
                    if slot == UP[p]:
                        act.wait_ge(s["up_done"], PAIRS * f + p + 1)
                        wait(act, s["hid_lo_ready"], PAIRS * f + p)
                        for k in range(2):
                            last = nc.scalar.activation(hid[:, k * N:(k + 1) * N], side[2][:, k * N:(k + 1) * N],
                                                        ACT.Relu, scale=up_col[:, 2 * p + k:2 * p + k + 1])
                        last.then_inc(s["hid_ready"], 1)
                        act.wait_ge(s["hid_ready"], PAIRS * f + p + 1)
                        wait(act, s["dn_done"], PAIRS * f + p - 1)
                        split_hi(flat(hid_hi[:, p % 2]), hid[:], s["hid_hi_ready"])
                if slot == LTR2:
                    act.wait_ge(s["ltr2_done"], f + 1)
                    split_hi(flat(xh[:]), side[0][:], s["xh_ready"])
                if slot == QKV_Q:
                    act.wait_ge(s["q_done"], f + 1)
                    split_hi(flat(qh), side[2][:], s["qh_ready"], scale=float(D) ** -0.5)
                if slot == QKV_K:
                    act.wait_ge(s["k_done"], f + 1)
                    split_hi(flat3(kh[:, 1]), side[1][:], s["kh_ready"])
                if slot == QKV_V:
                    act.wait_ge(s["v_done"], f + 1)
                    split_hi(flat(vh[:, 1]), side[0][:], s["vh_ready"])
                if slot == SCORE:
                    act.wait_ge(s["negmax_ready"], f + 1)
                    for b in range(G):
                        last = nc.scalar.activation(prob[:, b].rearrange("p k t -> p (k t)"),
                                                    side[2][:, b * 2 * T:(b + 1) * 2 * T], ACT.Exp,
                                                    bias=row_max[:, 1, b:b + 1], accum_out=row_sum[:, b:b + 1])
                    last.then_inc(s["exp_p_done"], 1)
                if slot == PTR:
                    act.wait_ge(s["ptr_done"], f + 1)
                    split_hi(flat3(pth), side[1][:], s["pth_ready"])
                if slot == PV:
                    act.wait_ge(s["pv_done"], f + 1)
                    act.wait_ge(s["rowinv_ready"], f + 1)
                    for b in range(G):
                        last = nc.scalar.activation(att[:, b], side[0][:, b * D:(b + 1) * D], ACT.Copy,
                                                    scale=row_inv[:, b:b + 1])
                    last.then_inc(s["att_scaled"], 1)
                if slot == OTR:
                    act.wait_ge(s["otr_done"], f + 1)
                    split_hi(flat(oh), side[2][:], s["oh_ready"])
                if slot == LTR3:
                    act.wait_ge(s["ltr3_done"], f + 1)
                    split_hi(flat(xmh[:]), side[0][:], s["xmh_ready"])

            def split_piece(n):
                act.wait_ge(landed[n % RING], 16 * (n // RING + 1))
                split_hi(splits[n - SIGNS][0], work[:, n % RING].rearrange("p (c n) -> p c n", c=2), s["split_hi_done"])

            def passage(g, experts, layer, wkv):
                for slot in range(SLOTS):
                    if experts:
                        expert_slot(g, slot)
                    if wkv:
                        wkv_slot(g + 2, slot)
                    if layer:
                        layer_slot(g + 1, slot)
                    if not experts and SIGNS <= piece_of(layer, slot) < len(pieces):
                        split_piece(piece_of(layer, slot))

            act.wait_ge(s["chan_step"], 1)
            nc.scalar.activation(chan[:, 5], chan[:, 5], ACT.Exp).then_inc(s["chan_step"], 1)
            act.wait_ge(s["ld_gates"], 48)
            nc.scalar.activation(gates[:], gates_raw[:, 0:4], ACT.Tanh).then_inc(s["gates_ready"], 1)
            passage(-2, False, False, True)
            act.wait_ge(s["ld_upcol"], 16)
            act.wait_ge(s["ld_gatew"], 16)
            split_hi(flat(gate_hi[:]), flat(gate_raw[:]), s["gate_hi_ready"])
            passage(-1, False, True, True)
            passage(0, True, True, True)
            with act.Fori(1, NG - 2) as g:
                passage(g, True, True, True)
            passage(NG - 2, True, True, False)
            passage(NG - 1, True, False, False)

        @block.gpsimd
        def _(pool):
            def rstd(mv, rv, step, ready_in, count, ready):
                pool.wait_ge(ready_in, count)
                nc.gpsimd.tensor_tensor(rv[:, 0], mv[:, :, 1], eps[:], ALU.add).then_inc(step, 1)
                pool.wait_ge(step, count)
                nc.gpsimd.tensor_tensor(rv[:, 1], rv[:, 0], minus_half[:], ALU.pow).then_inc(ready, 1)

            def expert_slot(g, slot):
                e, part = divmod(slot, 3)
                if slot < 3 * NE and part == 1:
                    pool.wait_ge(s["ghi_ready"], NE * g + e + 1)
                    nc.gpsimd.tensor_tensor(flat(gated_lo[:, e % 2]), act_buf[:, e % 2], flat(f32(gated_hi[:, e % 2])),
                                            ALU.subtract).then_inc(s["glo_ready"], 1)

            def wkv_slot(g, slot):
                if slot == 0:
                    rstd(mv_w, rstd_w, s["w_rv"], s["w_mv"], g + 1, s["w_rstd"])
                if slot == 1:
                    pool.wait_ge(s["w_norm"], g + 1)
                    for b in range(G):
                        last = nc.gpsimd.tensor_tensor(xwn[:, b], xwn[:, b], ramp[:], ALU.add)
                    last.then_inc(s["w_ramped"], 1)
                if slot == KTR + 2:
                    pool.wait_ge(s["den_ready"], g + 1)
                    nc.gpsimd.tensor_tensor(flat3(eb[:]), flat3(eb[:]), flat3(vT[:]), ALU.mult).then_inc(s["ebv_ready"], 1)
                    pool.wait_ge(s["ebv_ready"], g + 1)
                    pool.wait_ge(s["p_scanned"], g + 1)
                    nc.gpsimd.tensor_tensor(p_late, p_late, flat3(eb[:]), ALU.add).then_inc(s["num_ready"], 1)
                if slot == YTR:
                    rstd(mv_1, rstd_1, s["rv1_step"], s["mv1_step"], g + 1, s["rstd1_ready"])

            def layer_slot(f, slot):
                if slot == DN[-1]:
                    rstd(mv_f, rstd_f, s["f_rv"], s["f_mv"], 2 * f + 1, s["f_rstd"])
                if slot == WO:
                    rstd(mv_f, rstd_f, s["f_rv"], s["f_mv"], 2 * f + 2, s["f_rstd"])
                for p in range(PAIRS):
                    if slot == UP[p]:
                        pool.wait_ge(s["hid_hi_ready"], PAIRS * f + p + 1)
                        nc.gpsimd.tensor_tensor(flat(hid_lo[:, p % 2]), hid[:], flat(f32(hid_hi[:, p % 2])),
                                                ALU.subtract).then_inc(s["hid_lo_ready"], 1)
                if slot == UP[-1]:
                    pool.wait_ge(s["kc_hi"], f + 1)
                    nc.gpsimd.tensor_tensor(flat3(kl[:, 0]), flat3(ctxT_a[:]), flat3(f32(kh[:, 0])),
                                            ALU.subtract).then_inc(s["kc_lo"], 1)
                    pool.wait_ge(s["vc_hi"], f + 1)
                    nc.gpsimd.tensor_tensor(flat(vl[:, 0]), flat(ctx_a[:]), flat(f32(vh[:, 0])),
                                            ALU.subtract).then_inc(s["vc_lo"], 1)

            def split_piece(n):
                hi, lo = splits[n - SIGNS]
                pool.wait_ge(s["split_hi_done"], n - SIGNS + 1)
                nc.gpsimd.tensor_tensor(lo, work[:, n % RING].rearrange("p (c n) -> p c n", c=2), f32(hi),
                                        ALU.subtract).then_inc(s["split_lo_done"], 1)

            def passage(g, experts, layer, wkv):
                for slot in range(SLOTS):
                    if experts:
                        expert_slot(g, slot)
                    if wkv:
                        wkv_slot(g + 2, slot)
                    if layer:
                        layer_slot(g + 1, slot)
                    if not experts and SIGNS <= piece_of(layer, slot) < len(pieces):
                        split_piece(piece_of(layer, slot))

            nc.gpsimd.memset(minus_half[:], -0.5).then_inc(s["consts_pool"], 1)
            nc.gpsimd.memset(eps[:], EPS).then_inc(s["consts_pool"], 1)
            nc.gpsimd.iota(time_col[:], pattern=[[0, 1]], base=0, channel_multiplier=-1,
                           allow_small_or_imprecise_dtypes=True).then_inc(s["consts_pool"], 1)
            nc.gpsimd.memset(ident[:], 0.0).then_inc(s["ident_ready"], 1)
            pool.wait_ge(s["ident_ready"], 1)
            nc.gpsimd.affine_select(out=ident[:], in_=ident[:], compare_op=ALU.not_equal, fill=1.0, base=0,
                                    pattern=[[-1, P]], channel_multiplier=1).then_inc(s["ident_ready"], 1)
            nc.gpsimd.memset(router_bias[:], NEVER).then_inc(s["bias_fill"], 1)
            nc.gpsimd.memset(gate_raw[:], 0.0).then_inc(s["bias_fill"], 1)
            nc.gpsimd.memset(earlier[:], 0.0).then_inc(s["consts_pool"], 1)
            pool.wait_ge(s["consts_pool"], 4)
            for e in range(1, NE):
                last = nc.gpsimd.memset(earlier[:, e, 0:e], 1.0)
            last.then_inc(s["consts_pool"], 1)
            pool.wait_ge(s["ramp_ready"], 1)
            passage(-2, False, False, True)
            pool.wait_ge(s["gate_hi_ready"], 1)
            nc.gpsimd.tensor_tensor(flat(gate_lo[:]), flat(gate_raw[:]), flat(f32(gate_hi[:])),
                                    ALU.subtract).then_inc(s["gate_lo_ready"], 1)
            passage(-1, False, True, True)
            passage(0, True, True, True)
            with pool.Fori(1, NG - 2) as g:
                passage(g, True, True, True)
            passage(NG - 2, True, True, False)
            passage(NG - 1, True, False, False)

        @block.vector
        def _(dve):
            def stats(src, stat, mv, stat_done, mv_done, count):
                for b in range(G):
                    last = nc.vector.bn_stats(stat[:, b], src[:, b])
                last.then_inc(stat_done, 1)
                dve.wait_ge(s["ident_ready"], 2)
                dve.wait_ge(stat_done, count)
                for b in range(G):
                    last = nc.vector.bn_aggr(mv[:, b], stat[:, b])
                last.then_inc(mv_done, 1)

            def normalise(dst, src, mv, rv, done):
                for b in range(G):
                    last = nc.vector.tensor_scalar(dst[:, b], src[:, b], mv[:, b, 0:1], rv[:, 1, b:b + 1],
                                                   ALU.subtract, ALU.mult)
                last.then_inc(done, 1)

            def split_lo(dst, src, hi, done):
                nc.vector.tensor_tensor(dst, src, hi, ALU.subtract).then_inc(done, 1)

            def router(g, slot):
                base = ROUTER_STEPS * g

                def step(k, ins):
                    ins.then_inc(s["r_step"], 1)
                    dve.wait_ge(s["r_step"], base + k)

                logits, expo, probs, biased, rank, chosen = (prb[:, i] for i in range(6))

                def by_expert(col):
                    return col.unsqueeze(2).to_broadcast([P, G, NE])

                def bias(i):
                    return router_bias[:, i].unsqueeze(1).to_broadcast([P, G, NE])

                if slot == GATE:
                    dve.wait_ge(s["logits_done"], g + 1)
                    step(1, nc.vector.tensor_tensor(logits, bank_out[:, 0:G * NE].rearrange("p (b e) -> p b e", b=G),
                                                    bias(0), ALU.add))
                    step(2, nc.vector.reduce_max(red[:, 0], logits, AX_X))
                    nc.vector.tensor_tensor(logits, logits, by_expert(red[:, 0]), ALU.subtract).then_inc(s["r_centred"], 1)
                if slot == GATE + 3:
                    dve.wait_ge(s["r_exp"], g + 1)
                    step(3, nc.vector.reduce_sum(red[:, 1], expo, AX_X))
                    step(4, nc.vector.reciprocal(red[:, 2], red[:, 1]))
                    step(5, nc.vector.tensor_tensor(probs, expo, by_expert(red[:, 2]), ALU.mult))
                    step(6, nc.vector.tensor_tensor(biased, probs, bias(1), ALU.add))
                    other = biased.unsqueeze(2).to_broadcast([P, G, NE, NE])
                    own = biased.unsqueeze(3).to_broadcast([P, G, NE, NE])
                    step(7, nc.vector.tensor_tensor(cmp_gt[:], other, own, ALU.is_gt))
                    step(8, nc.vector.tensor_tensor(cmp_eq[:], other, own, ALU.is_equal))
                    step(9, nc.vector.tensor_tensor(cmp_eq[:], cmp_eq[:], earlier[:].unsqueeze(1).to_broadcast([P, G, NE, NE]),
                                                    ALU.mult))
                    step(10, nc.vector.tensor_tensor(cmp_gt[:], cmp_gt[:], cmp_eq[:], ALU.add))
                    step(11, nc.vector.reduce_sum(rank, cmp_gt[:], AX_X))
                    step(12, nc.vector.scalar_tensor_tensor(chosen, rank, float(TOP_K), probs, ALU.is_lt, ALU.mult))
                    step(13, nc.vector.reduce_sum(red[:, 3], chosen, AX_X))
                    step(14, nc.vector.reciprocal(red[:, 4], red[:, 3]))
                    step(15, nc.vector.tensor_scalar(red[:, 4], red[:, 4], half_gate[:], None, ALU.mult))
                    step(16, nc.vector.tensor_tensor(wgt[:], chosen, by_expert(red[:, 4]), ALU.mult))
                    nc.vector.tensor_copy(wgt[:, :, NE - 1], half_gate[:].to_broadcast([P, G])).then_inc(s["wgt_ready"], 1)

            def expert_slot(g, slot):
                e, part = divmod(slot, 3)
                if slot < 3 * NE and part == 0:
                    dve.wait_ge(s["tanh_done"], NE * g + e + 1)
                    nc.vector.scalar_tensor_tensor(act_buf[:, e % 2], act_buf[:, e % 2], 1.0, bank_h1[e % 2][:],
                                                   ALU.add, ALU.mult).then_inc(s["act_done"], 1)
                if slot < 3 * NE and part == 1:
                    dve.wait_ge(s["h2_done"], NE * g + e + 1)
                    dve.wait_ge(s["act_done"], NE * g + e + 1)
                    nc.vector.tensor_tensor(act_buf[:, e % 2], act_buf[:, e % 2], bank_h2[e % 2][:],
                                            ALU.mult).then_inc(s["gated_ready"], 1)
                d = e - 1
                if (part == 2 or slot == 3 * NE) and d >= 0:
                    dve.wait_ge(s["out_done"], NE * g + d + 1)
                    if d == 0:
                        dve.wait_ge(s["wgt_ready"], g + 1)
                        wait(dve, s["stored"], 16 * g)
                    else:
                        dve.wait_ge(s["acc_done"], NE * g + d)
                    for b in range(G):
                        last = nc.vector.scalar_tensor_tensor(acc[:, b], bank_out[:, b * D:(b + 1) * D], wgt[:, b, d:d + 1],
                                                              (x23 if d == 0 else acc)[:, b], ALU.mult, ALU.add)
                    last.then_inc(s["acc_done"], 1)
                router(g, slot)

            def wkv_slot(g, slot):
                if slot == 0:
                    dve.wait_ge(s["ld_x"], 16 * (g + 1))
                    stats(xw, stat_w, mv_w, s["w_stat"], s["w_mv"], g + 1)
                if slot == 1:
                    dve.wait_ge(s["w_rstd"], g + 1)
                    normalise(xwn, xw, mv_w, rstd_w, s["w_norm"])
                if slot == KTR + 1:
                    dve.wait_ge(s["exp_done"], g + 1)
                    nc.vector.tensor_tensor_scan(q_state[:, 1:], flat3(decay[:]), flat3(ea[:]), 0.0, ALU.mult,
                                                 ALU.add).then_inc(s["q_scanned"], 1)
                    dve.wait_ge(s["q_scanned"], g + 1)
                    nc.vector.tensor_tensor(q_late, q_late, flat3(eb[:]), ALU.add).then_inc(s["den_ready"], 1)
                if slot == KTR + 2:
                    dve.wait_ge(s["ld_v"], 16 * C * (g + 1))
                    nc.vector.tensor_tensor(flat3(ea[:]), flat3(ea[:]), flat3(vT[:]), ALU.mult).then_inc(s["eav_ready"], 1)
                    dve.wait_ge(s["eav_ready"], g + 1)
                    nc.vector.tensor_tensor_scan(p_state[:, 1:], flat3(decay[:]), flat3(ea[:]), 0.0, ALU.mult,
                                                 ALU.add).then_inc(s["p_scanned"], 1)
                for i in range(2):
                    if slot == KTR + 4 + i:
                        if i == 0:
                            dve.wait_ge(s["den_ready"], g + 1)
                        half = q_state[:, i * N:(i + 1) * N]
                        nc.vector.reciprocal(half, half).then_inc(s["den_inv"], 1)
                if slot == KTR + 7:
                    dve.wait_ge(s["num_ready"], g + 1)
                    dve.wait_ge(s["den_inv"], 2 * g + 2)
                    nc.vector.tensor_tensor(flat3(ea[:]), p_late, q_late, ALU.mult).then_inc(s["y_raw"], 1)
                    dve.wait_ge(s["y_raw"], g + 1)
                    nc.vector.tensor_copy(ea[:, :, :, 0], vT[:, :, :, 0]).then_inc(s["y_ready"], 1)
                if slot == YTR:
                    dve.wait_ge(s["ytr_done"], g + 1)
                    nc.vector.scalar_tensor_tensor(flat(x1[:]), side[1][:], gates[:, 0:1], flat(xw[:]), ALU.mult,
                                                   ALU.add).then_inc(s["x1_ready"], 1)
                    dve.wait_ge(s["x1_ready"], g + 1)
                    stats(x1, stat_1, mv_1, s["stat1_step"], s["mv1_step"], g + 1)

            def layer_slot(f, slot):
                if slot == 0:
                    dve.wait_ge(s["rstd1_ready"], f + 1)
                    wait(dve, s["ltr3_done"], f)
                    normalise(xfn, x1, mv_1, rstd_1, s["xn_ready"])
                if slot == LTR1:
                    dve.wait_ge(s["xh_ready"], 2 * f + 1)
                    split_lo(flat(xl[:]), side[0][:], flat(f32(xh[:])), s["xl_ready"])
                if slot == DN[-1]:
                    dve.wait_ge(s["dn_done"], PAIRS * f + PAIRS)
                    nc.vector.tensor_tensor(x23[:], side[1][:].rearrange("p (b d) -> p b d", b=G),
                                            down_row[:].unsqueeze(1).to_broadcast([P, G, D]), ALU.mult).then_inc(s["ffn_scaled"], 1)
                    dve.wait_ge(s["ffn_scaled"], f + 1)
                    nc.vector.tensor_tensor(x23[:], x23[:], x1[:], ALU.add).then_inc(s["x2_ready"], 1)
                    dve.wait_ge(s["x2_ready"], f + 1)
                    stats(x23, stat_f, mv_f, s["f_stat"], s["f_mv"], 2 * f + 1)
                if slot == DN[-1] + 1:
                    dve.wait_ge(s["f_rstd"], 2 * f + 1)
                    normalise(xfn, x23, mv_f, rstd_f, s["xn_ready"])
                if slot == LTR2:
                    dve.wait_ge(s["xh_ready"], 2 * f + 2)
                    split_lo(flat(xl[:]), side[0][:], flat(f32(xh[:])), s["xl_ready"])
                if slot == QKV_Q:
                    dve.wait_ge(s["qh_ready"], f + 1)
                    nc.vector.scalar_tensor_tensor(flat(ql), side[2][:], float(D) ** -0.5, flat(f32(qh)), ALU.mult,
                                                   ALU.subtract).then_inc(s["ql_ready"], 1)
                if slot == QKV_K:
                    dve.wait_ge(s["kh_ready"], f + 1)
                    split_lo(flat3(kl[:, 1]), side[1][:], flat3(f32(kh[:, 1])), s["kl_ready"])
                if slot == QKV_V:
                    dve.wait_ge(s["vh_ready"], f + 1)
                    split_lo(flat(vl[:, 1]), side[0][:], flat(f32(vh[:, 1])), s["vl_ready"])
                if slot == SCORE:
                    dve.wait_ge(s["score_done"], f + 1)
                    nc.vector.reduce_max(row_max[:, 0], side[2][:].rearrange("p (b k) -> p b k", b=G), AX_X).then_inc(s["max_ready"], 1)
                    dve.wait_ge(s["max_ready"], f + 1)
                    nc.vector.tensor_scalar(row_max[:, 1], row_max[:, 0], -1.0, None, ALU.mult).then_inc(s["negmax_ready"], 1)
                if slot == PTR:
                    dve.wait_ge(s["exp_p_done"], f + 1)
                    nc.vector.reciprocal(row_inv[:], row_sum[:]).then_inc(s["rowinv_ready"], 1)
                    dve.wait_ge(s["pth_ready"], f + 1)
                    split_lo(flat3(ptl), side[1][:], flat3(f32(pth)), s["ptl_ready"])
                if slot == OTR:
                    dve.wait_ge(s["oh_ready"], f + 1)
                    split_lo(flat(ol), side[2][:], flat(f32(oh)), s["ol_ready"])
                if slot == WO:
                    dve.wait_ge(s["wo_done"], f + 1)
                    nc.vector.scalar_tensor_tensor(flat(x23[:]), side[1][:], gates[:, 1:2], flat(x23[:]), ALU.mult,
                                                   ALU.add).then_inc(s["x3_ready"], 1)
                    dve.wait_ge(s["x3_ready"], f + 1)
                    stats(x23, stat_f, mv_f, s["f_stat"], s["f_mv"], 2 * f + 2)
                if slot == WO + 1:
                    dve.wait_ge(s["f_rstd"], 2 * f + 2)
                    normalise(xfn, x23, mv_f, rstd_f, s["xn_ready"])
                if slot == LTR3:
                    dve.wait_ge(s["xmh_ready"], f + 1)
                    split_lo(flat(xml[:]), side[0][:], flat(f32(xmh[:])), s["xml_ready"])

            def sign_piece(n):
                dve.wait_ge(landed[n % RING], 16 * (n // RING + 1))
                raw = work[:, n % RING]
                wait(dve, s["sign_done"], n)
                nc.vector.tensor_scalar(hid[:], raw, 0.0, None, ALU.is_lt).then_inc(s["sign_neg"], 1)
                dve.wait_ge(s["sign_neg"], n + 1)
                nc.vector.scalar_tensor_tensor(signs[n], raw.rearrange("p (c n) -> p c n", c=2), 0.0,
                                               hid[:].rearrange("p (c n) -> p c n", c=2), ALU.is_gt,
                                               ALU.subtract).then_inc(s["sign_done"], 1)

            def passage(g, experts, layer, wkv):
                for slot in range(SLOTS):
                    if experts:
                        expert_slot(g, slot)
                    if wkv:
                        wkv_slot(g + 2, slot)
                    if layer:
                        layer_slot(g + 1, slot)
                    if not experts and piece_of(layer, slot) < SIGNS:
                        sign_piece(piece_of(layer, slot))

            w_col, u_col = wu[:, 0], wu[:, 1]
            dve.wait_ge(s["ld_wu"], 32)
            nc.vector.tensor_scalar(chan[:, 5], w_col, 0.0, None, ALU.min).then_inc(s["chan_step"], 1)
            dve.wait_ge(s["chan_step"], 2)
            nc.vector.tensor_scalar(chan[:, 0], w_col, 0.0, None, ALU.max).then_inc(s["chan_step"], 1)
            dve.wait_ge(s["chan_step"], 3)
            nc.vector.tensor_scalar(chan[:, 1], chan[:, 0], -1.0, None, ALU.mult).then_inc(s["chan_step"], 1)
            dve.wait_ge(s["chan_step"], 4)
            nc.vector.tensor_tensor(chan[:, 2], chan[:, 1], u_col, ALU.max).then_inc(s["chan_step"], 1)
            dve.wait_ge(s["chan_step"], 5)
            nc.vector.tensor_tensor(chan[:, 3], chan[:, 1], chan[:, 2], ALU.subtract).then_inc(s["chan_step"], 1)
            nc.vector.tensor_tensor(chan[:, 4], u_col, chan[:, 2], ALU.subtract).then_inc(s["chan_step"], 1)
            dve.wait_ge(s["ld_ramp"], 16)
            dve.wait_ge(s["consts_pool"], 5)
            nc.vector.tensor_scalar(ramp[:], ramp[:], 0.0, time_col[:], ALU.max, ALU.mult).then_inc(s["ramp_ready"], 1)
            nc.vector.memset(decay[:], 1.0).then_inc(s["decay_step"], 1)
            dve.wait_ge(s["decay_step"], 1)
            for c in range(C):
                last = nc.vector.tensor_scalar(flat(decay[:, c]), flat(decay[:, c]), chan[:, 5, c:c + 1], None, ALU.mult)
            last.then_inc(s["decay_step"], 1)
            dve.wait_ge(s["decay_step"], 2)
            nc.vector.memset(decay[:, :, :, 0], 0.0).then_inc(s["decay_step"], 1)
            nc.vector.memset(q_state[:, 0:1], 1.0).then_inc(s["decay_step"], 1)
            dve.wait_ge(s["decay_step"], 4)
            dve.wait_ge(s["gates_ready"], 1)
            nc.vector.tensor_scalar(half_gate[:], gates[:, 3:4], 0.5, None, ALU.mult).then_inc(s["scales_ready"], 1)
            dve.wait_ge(s["ld_drow"], 16)
            nc.vector.tensor_scalar(down_row[:], down_row[:], gates_raw[:, 4:5], gates[:, 2:3], ALU.mult,
                                    ALU.mult).then_inc(s["scales_ready"], 1)
            dve.wait_ge(s["scales_ready"], 2)
            passage(-2, False, False, True)
            dve.wait_ge(s["ld_rbias"], 32)
            passage(-1, False, True, True)
            passage(0, True, True, True)
            with dve.Fori(1, NG - 2) as g:
                passage(g, True, True, True)
            passage(NG - 2, True, True, False)
            passage(NG - 1, True, False, False)


def kernel(**inputs):
    import numpy as _np
    import concourse.bacc as _bacc
    from concourse import mybir as _mybir
    from concourse.bass_utils import run_bass_kernel_spmd as _run

    layout = [
        ("x", inputs["x"]),
        ("ctx_in", inputs["ctx_2048"]),
        ("ctxT_in", _np.transpose(inputs["ctx_2048"], (0, 2, 1))),
        ("g_xattn", inputs["g_xattn"]), ("g_ffn", inputs["g_ffn"]),
        ("w_in", inputs["L0_xattn_w"]),
        ("w_cols", _np.transpose(inputs["L0_xattn_w"].reshape(-1, P))),
        ("u_cols", _np.transpose(inputs["L0_xattn_u"].reshape(-1, P))),
        ("upT_in", _np.transpose(inputs["L0_ffn_up_weight"])),
        ("downT_in", _np.transpose(inputs["L0_ffn_down_weight"])),
        ("up_cols", _np.transpose(inputs["L0_ffn_up_scale"].reshape(-1, P))),
         ("down_scale", inputs["L0_ffn_down_scale"]),
        ("output_scale", inputs["L0_ffn_output_scale"]),
        ("wqT_in", _np.transpose(inputs["L1_xattn_wq"])), ("wkT_in", _np.transpose(inputs["L1_xattn_wk"])),
        ("wvT_in", _np.transpose(inputs["L1_xattn_wv"])), ("woT_in", _np.transpose(inputs["L1_xattn_wo"])),
        ("W1", inputs["L1_ffn_W1"]), ("Wg", inputs["L1_ffn_Wg"]), ("W2", inputs["L1_ffn_W2"]),
        ("Ws1", inputs["L1_ffn_Ws1"]), ("Wsg", inputs["L1_ffn_Wsg"]), ("Ws2", inputs["L1_ffn_Ws2"]),
        ("gate_w", inputs["L1_ffn_gate_w"]), ("gate_b", inputs["L1_ffn_gate_b"]), ("biases", inputs["L1_ffn_biases"]),
    ]
    nc = _bacc.Bacc("TRN2", target_bir_lowering=False, num_devices=1)
    arrays, args = {}, {}
    for name, a in layout:
        a = _np.ascontiguousarray(a)
        arrays[f"in_{name}"] = a
        args[name] = nc.dram_tensor(f"in_{name}", a.shape, _mybir.dt.from_np(a.dtype), kind="ExternalInput").ap()
    args["out"] = nc.dram_tensor("out_0", inputs["x"].shape, _mybir.dt.float32, kind="ExternalOutput").ap()
    flamingo_kernel(nc, **args)
    return _run(nc, [arrays], core_ids=[0]).results[0]["out_0"]
```

```python
import concourse.bass as bass
from concourse import mybir
from contextlib import ExitStack

F32 = mybir.dt.float32
F32R = mybir.dt.float32r
ALU = mybir.AluOpType
ACT = mybir.ActivationFunctionType
AX_X = mybir.AxisListType.X

P = 128
EPS = 1e-5
NEVER = -1e30
TOP_K = 3
SLOTS = 25
RING = 3
ROUTER_STEPS = 16

AT = {
    "ktr_done": 7, "ytr_done": 14, "ltr1_done": 23,
    "exp_done": 8, "x1h_ready": 24,
    "stat0_done": 0, "mv0_done": 1, "norm0_done": 4, "q_scanned": 7, "den_ready": 8, "eav_ready": 8,
    "p_scanned": 11, "den_inv": (9, 12, 10, 10), "y_raw": 12, "y_ready": 12, "x1_ready": 13, "stat1_done": 13,
    "mv1_done": 16, "norm1_done": 22, "x1l_ready": 23,
    "var0_done": 2, "rstd0_done": 2, "ramp_added": 4, "ebv_ready": 8, "num_ready": 8, "var1_done": 15,
    "rstd1_done": 22,
    "up_done": (0, 1, 3, 4), "dn_done": (3, 4, 5, 6), "ltr2_done": 10, "q_done": 11, "k_done": 11, "v_done": 12,
    "score_done": 13, "ptr_done": 15, "pv_done": 17, "otr_done": 18, "wo_done": 19, "ltr3_done": 22,
    "hid_ready": (0, 0, 4, 5), "hid_hi_ready": (0, 2, 5, 5), "x2h_ready": 9, "qh_ready": 11, "kh_ready": 9,
    "vh_ready": 13, "kc_hi": 7, "vc_hi": 13, "exp_p_done": 14, "pth_ready": 15, "att_scaled": 16,
    "oh_ready": 16, "xmh_ready": 22,
    "ffn_scaled": 6, "x2_ready": 6, "stat2_done": 6, "mv2_done": 6, "norm2_done": 7, "x2l_ready": 8,
    "ql_ready": 11, "kl_ready": 11, "vl_ready": 14, "max_ready": 12, "negmax_ready": 12, "rowinv_ready": 15,
    "ptl_ready": 14, "ol_ready": 17, "x3_ready": 19, "stat3_done": 19, "mv3_done": 19, "norm3_done": 20,
    "xml_ready": 22,
    "hid_lo_ready": (0, 1, 2, 2), "var2_done": 5, "rstd2_done": 5, "kc_lo": 5, "vc_lo": 12, "var3_done": 17,
    "rstd3_done": 17,
    "r_exp": 1,
    "r_step": (0, 0, 1, 1, 1, 1, 1, 2, 2, 3, 3, 3, 3, 3, 3, 3), "r_centred": 0, "wgt_ready": 3,
}
EXPERT_AT = {"tanh_done": 0, "act_done": 0, "gated_ready": 1, "ghi_ready": 3, "glo_ready": 2, "acc_done": 5}


def flamingo_kernel(nc, x, ctx_in, ctxT_in, g_xattn, g_ffn, w_in, w_cols, u_cols, upT_in, downT_in, up_cols,
                    down_scale, output_scale, wqT_in, wkT_in, wvT_in, woT_in, W1, Wg, W2, Ws1, Wsg,
                    Ws2, gate_w, gate_b, biases, out):
    B, T, D = x.shape
    C = D // P
    H = upT_in.shape[1]
    M = H // P
    NE = W1.shape[0] + 1
    NR = W1.shape[0]
    G = 2
    NG = B // G
    N = G * T
    PAIRS = M // 2
    assert T == P and C == 2 and NE == 8 and N * 2 == 512

    ctx = ExitStack()
    with ctx:
        def sb(name, shape, dt=F32):
            return ctx.enter_context(nc.sbuf_tensor(name, shape, dt))

        def bank(name):
            return ctx.enter_context(nc.psum_tensor(name, [P, 512], F32))

        bank_h1 = [bank("h1_0"), bank("h1_1")]
        bank_h2 = [bank("h2_0"), bank("h2_1")]
        bank_out = bank("expert_out")
        side = [bank(f"side{i}") for i in range(3)]

        moe_hi = sb("moe_hi", [P, NE, 3, C, D], F32R)
        moe_lo = sb("moe_lo", [P, NE, 3, C, D], F32R)
        up_sign = sb("up_sign", [P, C, H], F32R)
        down_sign = sb("down_sign", [P, M, D], F32R)
        att_hi = sb("att_hi", [P, 4, C, D], F32R)
        att_lo = sb("att_lo", [P, 4, C, D], F32R)
        gate_raw = sb("gate_raw", [P, C, NE])
        gate_hi = sb("gate_hi", [P, C, NE], F32R)
        gate_lo = sb("gate_lo", [P, C, NE], F32R)

        ident = sb("ident", [P, P])
        wu = sb("wu", [P, 2, C])
        chan = sb("chan", [P, 6, C])
        decay = sb("decay", [P, C, G, T])
        ramp = sb("ramp", [P, D])
        time_col = sb("time_col", [P, 1])
        gates_raw = sb("gates_raw", [P, 5])
        gates = sb("gates", [P, 4])
        half_gate = sb("half_gate", [P, 1])
        down_row = sb("down_row", [P, D])
        up_col = sb("up_col", [P, M])
        router_bias = sb("router_bias", [P, 2, NE])
        earlier = sb("earlier", [P, NE, NE])
        minus_half = sb("minus_half", [P, G])
        eps = sb("eps", [P, G])
        scratch = sb("scratch", [P, 1])

        xw = sb("xw", [P, G, D])
        vT = sb("vT", [P, C, G, T])
        ea = sb("ea", [P, C, G, T])
        eb = sb("eb", [P, C, G, T])
        p_state = sb("p_state", [P, 1 + C * N])
        q_state = sb("q_state", [P, 1 + C * N])
        p_late, q_late = p_state[:, 0:C * N], q_state[:, 0:C * N]
        xwn = p_late.rearrange("p (b d) -> p b d", b=G)
        stat_w = sb("stat_w", [P, G, 6])
        mv_w = sb("mv_w", [P, G, 2])
        rstd_w = sb("rstd_w", [P, 2, G])
        x1 = sb("x1", [P, G, D])
        stat_1 = sb("stat_1", [P, G, 6])
        mv_1 = sb("mv_1", [P, G, 2])
        rstd_1 = sb("rstd_1", [P, 2, G])
        x23 = sb("x23", [P, G, D])
        xfn = sb("xfn", [P, G, D])
        att = xfn
        stat_f = sb("stat_f", [P, G, 6])
        mv_f = sb("mv_f", [P, G, 2])
        rstd_f = sb("rstd_f", [P, 2, G])
        xh = sb("xh", [P, C, N], F32R)
        xl = sb("xl", [P, C, N], F32R)
        pth = xh[:].rearrange("p k (b t) -> p k b t", b=G)
        ptl = xl[:].rearrange("p k (b t) -> p k b t", b=G)
        hid = sb("hid", [P, 2, 2 * N])
        prob = hid[:, 0].rearrange("p (b k t) -> p b k t", b=G, k=2)
        hid_hi = sb("hid_hi", [P, 2, 2, N], F32R)
        hid_lo = sb("hid_lo", [P, 2, 2, N], F32R)
        qh, ql = hid_hi[:, 0], hid_lo[:, 0]
        oh, ol = hid_hi[:, 1], hid_lo[:, 1]
        ctxT_a = sb("ctxT_a", [P, C, G, T])
        ctx_a = sb("ctx_a", [P, G, D])
        kh = sb("kh", [P, 2, C, G, T], F32R)
        kl = sb("kl", [P, 2, C, G, T], F32R)
        vh = sb("vh", [P, 2, G, D], F32R)
        vl = sb("vl", [P, 2, G, D], F32R)
        row_max = sb("row_max", [P, 2, G])
        row_sum = sb("row_sum", [P, G])
        row_inv = sb("row_inv", [P, G])
        xmh = sb("xmh", [P, C, N], F32R)
        xml = sb("xml", [P, C, N], F32R)
        work = sb("work", [P, 3, C * N])
        act_buf = work[:, 0:2]
        acc = work[:, 2].rearrange("p (b d) -> p b d", b=G)
        gated_hi = sb("gated_hi", [P, 2, C, N], F32R)
        gated_lo = sb("gated_lo", [P, 2, C, N], F32R)
        prb = sb("prb", [P, 6, G, NE])
        cmp_gt = sb("cmp_gt", [P, G, NE, NE])
        cmp_eq = sb("cmp_eq", [P, G, NE, NE])
        red = sb("red", [P, 5, G])
        wgt = sb("wgt", [P, G, NE])

        pieces = [upT_in.rearrange("(c p) h -> p c h", p=P)[:, :, j * D:(j + 1) * D] for j in range(H // D)]
        pieces += [downT_in.rearrange("(m p) d -> p m d", p=P)[:, 2 * j:2 * j + 2, :] for j in range(M // 2)]
        SIGNS = len(pieces)
        signs = [up_sign[:, :, j * D:(j + 1) * D] for j in range(H // D)]
        signs += [down_sign[:, 2 * j:2 * j + 2, :] for j in range(M // 2)]
        pieces += [w.rearrange("(c p) n -> p c n", p=P) for w in (wqT_in, wkT_in, wvT_in, woT_in)]
        splits = [(att_hi[:, i], att_lo[:, i]) for i in range(4)]
        LAYER_PIECES = len(pieces)
        for e in range(NE):
            for i, w in enumerate((W1[e], Wg[e], W2[e]) if e < NR else (Ws1, Wsg, Ws2)):
                pieces.append(w.rearrange("(c p) n -> p c n", p=P))
                splits.append((moe_hi[:, e, i], moe_lo[:, e, i]))

        names = """
        ld_x ld_v ld_ctxT ld_ctx ld_wu ld_ramp ld_gates ld_upcol ld_drow ld_gatew ld_rbias
        ld_piece0 ld_piece1 ld_piece2 stored
        ident_ready consts_pool bias_fill chan_step decay_step ramp_ready gates_ready scales_ready
        gate_hi_ready gate_lo_ready sign_neg sign_done split_hi_done split_lo_done
        stat0_done mv0_done var0_done rstd0_done norm0_done ramp_added ktr_done exp_done
        q_scanned den_ready den_inv eav_ready p_scanned ebv_ready num_ready y_raw y_ready ytr_done x1_ready
        stat1_done mv1_done var1_done rstd1_done norm1_done ltr1_done x1h_ready x1l_ready
        stat2_done mv2_done var2_done rstd2_done norm2_done ltr2_done x2h_ready x2l_ready
        stat3_done mv3_done var3_done rstd3_done norm3_done ltr3_done up_done hid_ready hid_hi_ready hid_lo_ready
        dn_done ffn_scaled x2_ready kc_hi kc_lo vc_hi vc_lo q_done k_done v_done qh_ready ql_ready kh_ready
        kl_ready vh_ready vl_ready score_done max_ready negmax_ready exp_p_done rowinv_ready ptr_done
        pth_ready ptl_ready pv_done att_scaled otr_done oh_ready ol_ready wo_done x3_ready
        xmh_ready xml_ready
        h1_done tanh_done act_done h2_done gated_ready ghi_ready glo_ready out_done acc_done
        logits_done r_step r_centred r_exp wgt_ready
        """.split()
        s = {n: ctx.enter_context(nc.semaphore(n)) for n in names}

        def wait(eng, sem, value):
            if not (isinstance(value, int) and value <= 0):
                eng.wait_ge(sem, value)

        x_g = x.rearrange("(g b) t d -> t (g b) d", b=G)
        out_g = out.rearrange("(g b) t d -> t (g b) d", b=G)
        ctx_g = ctx_in.rearrange("(g b) t d -> t (g b) d", b=G)
        ctxT_g = ctxT_in.rearrange("(g b) (c p) t -> p c (g b) t", b=G, p=P)

        def group(g):
            return bass.ds(g * G, G)

        def f32(ap):
            return ap.bitcast(F32)

        def flat(ap):
            return ap.rearrange("p a b -> p (a b)")

        def flat3(ap):
            return ap.rearrange("p a b c -> p (a b c)")

        landed = (s["ld_piece0"], s["ld_piece1"], s["ld_piece2"])

        def piece_of(layer, slot):
            if layer:
                return LAYER_PIECES + slot
            return slot - 1 if 1 <= slot <= LAYER_PIECES else len(pieces)

        block = ctx.enter_context(nc.Block())

        @block.sync
        def _(sp):
            def load_wkv(g):
                for c in range(C):
                    sp.dma_start(vT[:, c], ctxT_g[:, c, group(g), :]).then_inc(s["ld_v"], 16)
                sp.dma_start(xw[:], x_g[:, group(g), :]).then_inc(s["ld_x"], 16)

            def load_ctx(g):
                for c in range(C):
                    sp.dma_start(ctxT_a[:, c], ctxT_g[:, c, group(g), :]).then_inc(s["ld_ctxT"], 16)
                sp.dma_start(ctx_a[:], ctx_g[:, group(g), :]).then_inc(s["ld_ctx"], 16)

            def next_ctx(f):
                sp.wait_ge(s["kc_lo"], f + 1)
                sp.wait_ge(s["vc_lo"], f + 1)
                load_ctx(f + 1)

            def next_wkv(g):
                sp.wait_ge(s["x1_ready"], g + 1)
                load_wkv(g + 1)

            def store(g):
                sp.wait_ge(s["acc_done"], NE * g + NE)
                sp.dma_start(out_g[:, group(g), :], acc[:]).then_inc(s["stored"], 16)

            def load_piece(n):
                if n >= RING:
                    if n - RING < SIGNS:
                        sp.wait_ge(s["sign_done"], n - RING + 1)
                    else:
                        sp.wait_ge(s["split_lo_done"], n - RING - SIGNS + 1)
                sp.dma_start(work[:, n % RING].rearrange("p (c n) -> p c n", c=2), pieces[n]).then_inc(landed[n % RING], 16)

            sp.dma_start(xw[:], x_g[:, group(0), :]).then_inc(s["ld_x"], 16)
            sp.dma_start(wu[:, 0], w_cols).then_inc(s["ld_wu"], 16)
            sp.dma_start(wu[:, 1], u_cols).then_inc(s["ld_wu"], 16)
            sp.dma_start(ramp[:], w_in.rearrange("(a d) -> a d", a=1).to_broadcast([P, D])).then_inc(s["ld_ramp"], 16)
            for c in range(C):
                sp.dma_start(vT[:, c], ctxT_g[:, c, group(0), :]).then_inc(s["ld_v"], 16)
            for n in range(RING):
                load_piece(n)
            for i, g in enumerate((g_xattn, g_ffn)):
                sp.dma_start(gates_raw[:, 2 * i:2 * i + 2],
                             g.rearrange("(a d) -> a d", a=1).to_broadcast([P, 2])).then_inc(s["ld_gates"], 16)
            sp.dma_start(gates_raw[:, 4:5],
                         output_scale.rearrange("(a d) -> a d", a=1).to_broadcast([P, 1])).then_inc(s["ld_gates"], 16)
            sp.dma_start(down_row[:], down_scale.rearrange("(a d) -> a d", a=1).to_broadcast([P, D])).then_inc(s["ld_drow"], 16)
            sp.dma_start(up_col[:], up_cols).then_inc(s["ld_upcol"], 16)
            load_ctx(0)
            sp.wait_ge(s["bias_fill"], 2)
            for i, r in enumerate((gate_b, biases)):
                sp.dma_start(router_bias[:, i, 0:NR],
                             r.rearrange("(a d) -> a d", a=1).to_broadcast([P, NR])).then_inc(s["ld_rbias"], 16)
            sp.dma_start(gate_raw[:, :, 0:NR], gate_w.rearrange("(c p) e -> p c e", p=P)).then_inc(s["ld_gatew"], 16)
            for n in range(RING, LAYER_PIECES):
                load_piece(n)
            next_wkv(0)
            for n in range(LAYER_PIECES, len(pieces)):
                load_piece(n)
            next_ctx(0)
            next_wkv(1)
            with sp.Fori(0, NG - 3) as g:
                next_ctx(g + 1)
                next_wkv(g + 2)
                store(g)
            next_ctx(NG - 2)
            for g in range(NG - 3, NG):
                store(g)
            sp.wait_ge(s["stored"], 16 * NG)

        @block.tensor
        def _(pe):
            def transpose8(dst, src):
                for c in range(C):
                    for b in range(G):
                        last = nc.tensor.transpose(dst[:, (c * G + b) * P:(c * G + b + 1) * P],
                                                   src[:, b, c * P:(c + 1) * P], ident[:])
                return last

            def three_pass(dst, pairs):
                steps = [ops for (ah, al), (bh, bl) in pairs for ops in ((ah, bh), (al, bh), (ah, bl))]
                for i, (a, b) in enumerate(steps):
                    last = nc.tensor.matmul(dst, a, b, start=(i == 0), stop=(i == len(steps) - 1))
                return last

            def weights_by_tokens(dst, hi, lo, col0, mh, ml):
                for n in range(2):
                    cols = slice(col0 + n * P, col0 + (n + 1) * P)
                    last = three_pass(dst[:, n * N:(n + 1) * N],
                                      [((hi[:, d, cols], lo[:, d, cols]), (mh[:, d], ml[:, d])) for d in range(C)])
                return last

            def tokens_by_weights(dst, mh, ml, hi, lo):
                for b in range(G):
                    tok = slice(b * P, (b + 1) * P)
                    last = three_pass(dst[:, b * D:(b + 1) * D],
                                      [((mh[:, d, tok], ml[:, d, tok]), (hi[:, d], lo[:, d])) for d in range(C)])
                return last

            def expert_slot(g, slot):
                e, part = divmod(slot, 3)
                if slot < 3 * NE and part == 0:
                    if e == 0:
                        pe.wait_ge(s["xmh_ready"], g + 1)
                        pe.wait_ge(s["xml_ready"], g + 1)
                    wait(pe, s["act_done"], NE * g + max(e - 1, 0))
                    weights_by_tokens(bank_h1[e % 2], moe_hi[:, e, 0], moe_lo[:, e, 0], 0, xmh, xml).then_inc(s["h1_done"], 1)
                elif slot < 3 * NE and part == 1:
                    wait(pe, s["gated_ready"], NE * g + max(e - 1, 0))
                    weights_by_tokens(bank_h2[e % 2], moe_hi[:, e, 1], moe_lo[:, e, 1], 0, xmh, xml).then_inc(s["h2_done"], 1)
                    if slot == 1:
                        wait(pe, s["acc_done"], NE * g)
                        for b in range(G):
                            tok = slice(b * P, (b + 1) * P)
                            last = three_pass(bank_out[:, b * NE:(b + 1) * NE],
                                              [((xmh[:, d, tok], xml[:, d, tok]), (gate_hi[:, d], gate_lo[:, d]))
                                               for d in range(C)])
                        last.then_inc(s["logits_done"], 1)
                else:
                    d = e - 1
                    if d < 0:
                        return
                    pe.wait_ge(s["glo_ready"], NE * g + d + 1)
                    if d == 0:
                        pe.wait_ge(s["r_step"], ROUTER_STEPS * g + 1)
                    else:
                        pe.wait_ge(s["acc_done"], NE * g + d)
                    tokens_by_weights(bank_out, gated_hi[:, d % 2], gated_lo[:, d % 2],
                                      moe_hi[:, d, 2], moe_lo[:, d, 2]).then_inc(s["out_done"], 1)

            def wkv_slot(g, slot):
                if slot == AT["ktr_done"]:
                    pe.wait_ge(s["ramp_added"], g + 1)
                    wait(pe, s["xmh_ready"], g - 1)
                    wait(pe, s["xml_ready"], g - 1)
                    transpose8(side[0], xwn).then_inc(s["ktr_done"], 1)
                if slot == AT["ytr_done"]:
                    pe.wait_ge(s["y_ready"], g + 1)
                    wait(pe, s["kh_ready"], g)
                    wait(pe, s["kl_ready"], g)
                    for b in range(G):
                        for c in range(C):
                            last = nc.tensor.transpose(side[1][:, b * D + c * P:b * D + (c + 1) * P],
                                                       ea[:, c, b], ident[:])
                    last.then_inc(s["ytr_done"], 1)
                if slot == AT["ltr1_done"]:
                    pe.wait_ge(s["norm1_done"], g + 1)
                    wait(pe, s["ol_ready"], g)
                    transpose8(side[2], xfn).then_inc(s["ltr1_done"], 1)

            def layer_slot(f, slot, beside_wkv):
                for p in range(PAIRS):
                    if slot == AT["up_done"][p]:
                        if p == 0:
                            pe.wait_ge(s["x1h_ready"], f + 1)
                            pe.wait_ge(s["x1l_ready"], f + 1)
                        else:
                            pe.wait_ge(s["hid_ready"], PAIRS * f + p)
                        for k in range(2):
                            m = 2 * p + k
                            for i, (d, part) in enumerate([(d, part) for d in range(C) for part in (xh, xl)]):
                                last = nc.tensor.matmul(side[2][:, k * N:(k + 1) * N], up_sign[:, d, m * P:(m + 1) * P],
                                                        part[:, d], start=(i == 0), stop=(i == 2 * C - 1))
                        last.then_inc(s["up_done"], 1)
                    if slot == AT["dn_done"][p]:
                        pe.wait_ge(s["hid_lo_ready"], PAIRS * f + p + 1)
                        for k in range(2):
                            for b in range(G):
                                for part in (hid_hi, hid_lo):
                                    last = nc.tensor.matmul(
                                        side[1][:, b * D:(b + 1) * D], part[:, p % 2, k, b * P:(b + 1) * P],
                                        down_sign[:, 2 * p + k],
                                        start=(p == 0 and k == 0 and b == 0 and part is hid_hi),
                                        stop=(p == PAIRS - 1 and k == 1 and part is hid_lo), skip_group_check=True)
                        last.then_inc(s["dn_done"], 1)
                if slot == AT["ltr2_done"]:
                    pe.wait_ge(s["norm2_done"], f + 1)
                    if beside_wkv:
                        pe.wait_ge(s["exp_done"], f + 2)
                    transpose8(side[0], xfn).then_inc(s["ltr2_done"], 1)
                if slot == AT["q_done"]:
                    pe.wait_ge(s["x2h_ready"], f + 1)
                    pe.wait_ge(s["x2l_ready"], f + 1)
                    weights_by_tokens(side[2], att_hi[:, 0], att_lo[:, 0], 0, xh, xl).then_inc(s["q_done"], 1)
                if slot == AT["k_done"]:
                    weights_by_tokens(side[1], att_hi[:, 1], att_lo[:, 1], 0, xh, xl).then_inc(s["k_done"], 1)
                if slot == AT["v_done"]:
                    tokens_by_weights(side[0], xh, xl, att_hi[:, 2], att_lo[:, 2]).then_inc(s["v_done"], 1)
                if slot == AT["score_done"]:
                    for ready in (s["qh_ready"], s["ql_ready"], s["kh_ready"], s["kl_ready"], s["kc_lo"]):
                        pe.wait_ge(ready, f + 1)
                    for b in range(G):
                        tok = slice(b * P, (b + 1) * P)
                        last = three_pass(side[2][:, b * 2 * T:(b + 1) * 2 * T],
                                          [((qh[:, c, tok], ql[:, c, tok]), (kh[:, :, c, b], kl[:, :, c, b]))
                                           for c in range(C)])
                    last.then_inc(s["score_done"], 1)
                if slot == AT["ptr_done"]:
                    pe.wait_ge(s["exp_p_done"], f + 1)
                    if beside_wkv:
                        pe.wait_ge(s["x1_ready"], f + 2)
                    for part in range(2):
                        for b in range(G):
                            last = nc.tensor.transpose(side[1][:, (part * G + b) * P:(part * G + b + 1) * P],
                                                       prob[:, b, part], ident[:])
                    last.then_inc(s["ptr_done"], 1)
                if slot == AT["pv_done"]:
                    for ready in (s["pth_ready"], s["ptl_ready"], s["vh_ready"], s["vl_ready"], s["vc_lo"]):
                        pe.wait_ge(ready, f + 1)
                    for b in range(G):
                        last = three_pass(side[0][:, b * D:(b + 1) * D],
                                          [((pth[:, part, b], ptl[:, part, b]), (vh[:, part, b], vl[:, part, b]))
                                           for part in range(2)])
                    last.then_inc(s["pv_done"], 1)
                if slot == AT["otr_done"]:
                    pe.wait_ge(s["att_scaled"], f + 1)
                    transpose8(side[2], att).then_inc(s["otr_done"], 1)
                if slot == AT["wo_done"]:
                    pe.wait_ge(s["oh_ready"], f + 1)
                    pe.wait_ge(s["ol_ready"], f + 1)
                    tokens_by_weights(side[1], oh, ol, att_hi[:, 3], att_lo[:, 3]).then_inc(s["wo_done"], 1)
                if slot == AT["ltr3_done"]:
                    pe.wait_ge(s["norm3_done"], f + 1)
                    transpose8(side[0], xfn).then_inc(s["ltr3_done"], 1)

            def passage(g, experts, layer, wkv):
                for slot in range(SLOTS):
                    if experts:
                        expert_slot(g, slot)
                    if wkv:
                        wkv_slot(g + 2, slot)
                    if layer:
                        layer_slot(g + 1, slot, wkv)

            pe.wait_ge(s["ident_ready"], 2)
            passage(-2, False, False, True)
            pe.wait_ge(s["sign_done"], SIGNS)
            pe.wait_ge(s["split_lo_done"], LAYER_PIECES - SIGNS)
            passage(-1, False, True, True)
            pe.wait_ge(s["gate_lo_ready"], 1)
            pe.wait_ge(s["split_lo_done"], len(splits))
            passage(0, True, True, True)
            with pe.Fori(1, NG - 2) as g:
                passage(g, True, True, True)
            passage(NG - 2, True, True, False)
            passage(NG - 1, True, False, False)

        @block.scalar
        def _(act):
            def expert_slot(g, slot):
                for e in range(NE):
                    if slot == 3 * e + EXPERT_AT["tanh_done"]:
                        act.wait_ge(s["h1_done"], NE * g + e + 1)
                        wait(act, s["glo_ready"], NE * g + max(e - 1, 0))
                        nc.scalar.activation(act_buf[:, e % 2], bank_h1[e % 2][:], ACT.Tanh, scale=0.5).then_inc(s["tanh_done"], 1)
                    if slot == 3 * e + EXPERT_AT["ghi_ready"]:
                        act.wait_ge(s["gated_ready"], NE * g + e + 1)
                        wait(act, s["out_done"], NE * g + max(e - 1, 0))
                        nc.scalar.activation(flat(gated_hi[:, e % 2]), act_buf[:, e % 2], ACT.Copy).then_inc(s["ghi_ready"], 1)
                if slot == AT["r_exp"]:
                    act.wait_ge(s["r_centred"], g + 1)
                    nc.scalar.activation(prb[:, 1], prb[:, 0], ACT.Exp).then_inc(s["r_exp"], 1)

            def split_hi(dst, src, done, scale=1.0):
                nc.scalar.activation(dst, src, ACT.Copy, scale=scale).then_inc(done, 1)

            def wkv_slot(g, slot):
                if slot == AT["exp_done"]:
                    act.wait_ge(s["ktr_done"], g + 1)
                    if isinstance(g, int) and g == 0:
                        act.wait_ge(s["chan_step"], 7)
                    for dst, row in ((ea, 3), (eb, 4)):
                        for c in range(C):
                            last = nc.scalar.activation(flat(dst[:, c]), side[0][:, c * N:(c + 1) * N], ACT.Exp,
                                                        bias=chan[:, row, c:c + 1])
                    last.then_inc(s["exp_done"], 1)
                if slot == AT["x1h_ready"]:
                    act.wait_ge(s["ltr1_done"], g + 1)
                    split_hi(flat(xh[:]), side[2][:], s["x1h_ready"])

            def layer_slot(f, slot):
                for p in range(PAIRS):
                    if slot == AT["hid_ready"][p]:
                        act.wait_ge(s["up_done"], PAIRS * f + p + 1)
                        wait(act, s["hid_lo_ready"], PAIRS * f + p - 1)
                        for k in range(2):
                            last = nc.scalar.activation(hid[:, p % 2, k * N:(k + 1) * N], side[2][:, k * N:(k + 1) * N],
                                                        ACT.Relu, scale=up_col[:, 2 * p + k:2 * p + k + 1])
                        last.then_inc(s["hid_ready"], 1)
                    if slot == AT["hid_hi_ready"][p]:
                        act.wait_ge(s["hid_ready"], PAIRS * f + p + 1)
                        wait(act, s["dn_done"], PAIRS * f + p - 1)
                        split_hi(flat(hid_hi[:, p % 2]), hid[:, p % 2], s["hid_hi_ready"])
                if slot == AT["x2h_ready"]:
                    act.wait_ge(s["ltr2_done"], f + 1)
                    split_hi(flat(xh[:]), side[0][:], s["x2h_ready"])
                if slot == AT["qh_ready"]:
                    act.wait_ge(s["q_done"], f + 1)
                    split_hi(flat(qh), side[2][:], s["qh_ready"], scale=float(D) ** -0.5)
                if slot == AT["kh_ready"]:
                    act.wait_ge(s["k_done"], f + 1)
                    split_hi(flat3(kh[:, 1]), side[1][:], s["kh_ready"])
                if slot == AT["vh_ready"]:
                    act.wait_ge(s["v_done"], f + 1)
                    split_hi(flat(vh[:, 1]), side[0][:], s["vh_ready"])
                if slot == AT["kc_hi"]:
                    act.wait_ge(s["ld_ctxT"], 16 * C * (f + 1))
                    wait(act, s["score_done"], f)
                    split_hi(flat3(kh[:, 0]), flat3(ctxT_a[:]), s["kc_hi"])
                if slot == AT["vc_hi"]:
                    act.wait_ge(s["ld_ctx"], 16 * (f + 1))
                    wait(act, s["pv_done"], f)
                    split_hi(flat(vh[:, 0]), flat(ctx_a[:]), s["vc_hi"])
                if slot == AT["exp_p_done"]:
                    act.wait_ge(s["negmax_ready"], f + 1)
                    for b in range(G):
                        last = nc.scalar.activation(prob[:, b].rearrange("p k t -> p (k t)"),
                                                    side[2][:, b * 2 * T:(b + 1) * 2 * T], ACT.Exp,
                                                    bias=row_max[:, 1, b:b + 1], accum_out=row_sum[:, b:b + 1])
                    last.then_inc(s["exp_p_done"], 1)
                if slot == AT["pth_ready"]:
                    act.wait_ge(s["ptr_done"], f + 1)
                    split_hi(flat3(pth), side[1][:], s["pth_ready"])
                if slot == AT["att_scaled"]:
                    act.wait_ge(s["pv_done"], f + 1)
                    act.wait_ge(s["rowinv_ready"], f + 1)
                    for b in range(G):
                        last = nc.scalar.activation(att[:, b], side[0][:, b * D:(b + 1) * D], ACT.Copy,
                                                    scale=row_inv[:, b:b + 1])
                    last.then_inc(s["att_scaled"], 1)
                if slot == AT["oh_ready"]:
                    act.wait_ge(s["otr_done"], f + 1)
                    split_hi(flat(oh), side[2][:], s["oh_ready"])
                if slot == AT["xmh_ready"]:
                    act.wait_ge(s["ltr3_done"], f + 1)
                    split_hi(flat(xmh[:]), side[0][:], s["xmh_ready"])

            def split_piece(n):
                act.wait_ge(landed[n % RING], 16 * (n // RING + 1))
                split_hi(splits[n - SIGNS][0], work[:, n % RING].rearrange("p (c n) -> p c n", c=2), s["split_hi_done"])

            def passage(g, experts, layer, wkv):
                for slot in range(SLOTS):
                    if experts:
                        expert_slot(g, slot)
                    if wkv:
                        wkv_slot(g + 2, slot)
                    if layer:
                        layer_slot(g + 1, slot)
                    if not experts and SIGNS <= piece_of(layer, slot) < len(pieces):
                        split_piece(piece_of(layer, slot))

            act.wait_ge(s["chan_step"], 1)
            nc.scalar.activation(chan[:, 5], chan[:, 5], ACT.Exp).then_inc(s["chan_step"], 1)
            act.wait_ge(s["ld_gates"], 48)
            nc.scalar.activation(gates[:], gates_raw[:, 0:4], ACT.Tanh).then_inc(s["gates_ready"], 1)
            passage(-2, False, False, True)
            act.wait_ge(s["ld_upcol"], 16)
            act.wait_ge(s["ld_gatew"], 16)
            split_hi(flat(gate_hi[:]), flat(gate_raw[:]), s["gate_hi_ready"])
            passage(-1, False, True, True)
            passage(0, True, True, True)
            with act.Fori(1, NG - 2) as g:
                passage(g, True, True, True)
            passage(NG - 2, True, True, False)
            passage(NG - 1, True, False, False)

        @block.gpsimd
        def _(pool):
            def add_eps(mv, rv, i, count):
                pool.wait_ge(s[f"mv{i}_done"], count)
                nc.gpsimd.tensor_tensor(rv[:, 0], mv[:, :, 1], eps[:], ALU.add).then_inc(s[f"var{i}_done"], 1)

            def rstd(rv, i, count):
                pool.wait_ge(s[f"var{i}_done"], count)
                nc.gpsimd.tensor_tensor(rv[:, 1], rv[:, 0], minus_half[:], ALU.pow).then_inc(s[f"rstd{i}_done"], 1)

            def expert_slot(g, slot):
                for e in range(NE):
                    if slot == 3 * e + EXPERT_AT["glo_ready"]:
                        pool.wait_ge(s["ghi_ready"], NE * g + e + 1)
                        nc.gpsimd.tensor_tensor(flat(gated_lo[:, e % 2]), act_buf[:, e % 2], flat(f32(gated_hi[:, e % 2])),
                                                ALU.subtract).then_inc(s["glo_ready"], 1)

            def wkv_slot(g, slot):
                if slot == AT["var0_done"]:
                    add_eps(mv_w, rstd_w, 0, g + 1)
                if slot == AT["rstd0_done"]:
                    rstd(rstd_w, 0, g + 1)
                if slot == AT["ramp_added"]:
                    pool.wait_ge(s["norm0_done"], g + 1)
                    for b in range(G):
                        last = nc.gpsimd.tensor_tensor(xwn[:, b], xwn[:, b], ramp[:], ALU.add)
                    last.then_inc(s["ramp_added"], 1)
                if slot == AT["ebv_ready"]:
                    pool.wait_ge(s["den_ready"], g + 1)
                    nc.gpsimd.tensor_tensor(flat3(eb[:]), flat3(eb[:]), flat3(vT[:]), ALU.mult).then_inc(s["ebv_ready"], 1)
                if slot == AT["num_ready"]:
                    pool.wait_ge(s["ebv_ready"], g + 1)
                    pool.wait_ge(s["p_scanned"], g + 1)
                    nc.gpsimd.tensor_tensor(p_late, p_late, flat3(eb[:]), ALU.add).then_inc(s["num_ready"], 1)
                if slot == AT["var1_done"]:
                    add_eps(mv_1, rstd_1, 1, g + 1)
                if slot == AT["rstd1_done"]:
                    rstd(rstd_1, 1, g + 1)

            def layer_slot(f, slot):
                for p in range(PAIRS):
                    if slot == AT["hid_lo_ready"][p]:
                        pool.wait_ge(s["hid_hi_ready"], PAIRS * f + p + 1)
                        nc.gpsimd.tensor_tensor(flat(hid_lo[:, p % 2]), hid[:, p % 2], flat(f32(hid_hi[:, p % 2])),
                                                ALU.subtract).then_inc(s["hid_lo_ready"], 1)
                for i in (2, 3):
                    if slot == AT[f"var{i}_done"]:
                        add_eps(mv_f, rstd_f, i, f + 1)
                    if slot == AT[f"rstd{i}_done"]:
                        rstd(rstd_f, i, f + 1)
                if slot == AT["kc_lo"]:
                    pool.wait_ge(s["kc_hi"], f + 1)
                    nc.gpsimd.tensor_tensor(flat3(kl[:, 0]), flat3(ctxT_a[:]), flat3(f32(kh[:, 0])),
                                            ALU.subtract).then_inc(s["kc_lo"], 1)
                if slot == AT["vc_lo"]:
                    pool.wait_ge(s["vc_hi"], f + 1)
                    nc.gpsimd.tensor_tensor(flat(vl[:, 0]), flat(ctx_a[:]), flat(f32(vh[:, 0])),
                                            ALU.subtract).then_inc(s["vc_lo"], 1)

            def split_piece(n):
                hi, lo = splits[n - SIGNS]
                pool.wait_ge(s["split_hi_done"], n - SIGNS + 1)
                nc.gpsimd.tensor_tensor(lo, work[:, n % RING].rearrange("p (c n) -> p c n", c=2), f32(hi),
                                        ALU.subtract).then_inc(s["split_lo_done"], 1)

            def passage(g, experts, layer, wkv):
                for slot in range(SLOTS):
                    if experts:
                        expert_slot(g, slot)
                    if wkv:
                        wkv_slot(g + 2, slot)
                    if layer:
                        layer_slot(g + 1, slot)
                    if not experts and SIGNS <= piece_of(layer, slot) < len(pieces):
                        split_piece(piece_of(layer, slot))

            nc.gpsimd.memset(minus_half[:], -0.5).then_inc(s["consts_pool"], 1)
            nc.gpsimd.memset(eps[:], EPS).then_inc(s["consts_pool"], 1)
            nc.gpsimd.iota(time_col[:], pattern=[[0, 1]], base=0, channel_multiplier=-1,
                           allow_small_or_imprecise_dtypes=True).then_inc(s["consts_pool"], 1)
            nc.gpsimd.memset(ident[:], 0.0).then_inc(s["ident_ready"], 1)
            pool.wait_ge(s["ident_ready"], 1)
            nc.gpsimd.affine_select(out=ident[:], in_=ident[:], compare_op=ALU.not_equal, fill=1.0, base=0,
                                    pattern=[[-1, P]], channel_multiplier=1).then_inc(s["ident_ready"], 1)
            nc.gpsimd.memset(router_bias[:], NEVER).then_inc(s["bias_fill"], 1)
            nc.gpsimd.memset(gate_raw[:], 0.0).then_inc(s["bias_fill"], 1)
            nc.gpsimd.memset(earlier[:], 0.0).then_inc(s["consts_pool"], 1)
            pool.wait_ge(s["consts_pool"], 4)
            for e in range(1, NE):
                last = nc.gpsimd.memset(earlier[:, e, 0:e], 1.0)
            last.then_inc(s["consts_pool"], 1)
            pool.wait_ge(s["ramp_ready"], 1)
            passage(-2, False, False, True)
            pool.wait_ge(s["gate_hi_ready"], 1)
            nc.gpsimd.tensor_tensor(flat(gate_lo[:]), flat(gate_raw[:]), flat(f32(gate_hi[:])),
                                    ALU.subtract).then_inc(s["gate_lo_ready"], 1)
            passage(-1, False, True, True)
            passage(0, True, True, True)
            with pool.Fori(1, NG - 2) as g:
                passage(g, True, True, True)
            passage(NG - 2, True, True, False)
            passage(NG - 1, True, False, False)

        @block.vector
        def _(dve):
            def stats(src, stat, i):
                for b in range(G):
                    last = nc.vector.bn_stats(stat[:, b], src[:, b])
                last.then_inc(s[f"stat{i}_done"], 1)

            def mean_var(stat, mv, i, count):
                dve.wait_ge(s[f"stat{i}_done"], count)
                nc.vector.memset(scratch[:], 0.0)
                for b in range(G):
                    last = nc.vector.bn_aggr(mv[:, b], stat[:, b])
                last.then_inc(s[f"mv{i}_done"], 1)

            def normalise(dst, src, mv, rv, i):
                for b in range(G):
                    last = nc.vector.tensor_scalar(dst[:, b], src[:, b], mv[:, b, 0:1], rv[:, 1, b:b + 1],
                                                   ALU.subtract, ALU.mult)
                last.then_inc(s[f"norm{i}_done"], 1)

            def split_lo(dst, src, hi, done):
                nc.vector.tensor_tensor(dst, src, hi, ALU.subtract).then_inc(done, 1)

            def router(g, slot):
                base = ROUTER_STEPS * g

                def due(k):
                    if slot == AT["r_step"][k - 1] and k > 1:
                        dve.wait_ge(s["r_step"], base + k - 1)
                    return slot == AT["r_step"][k - 1]

                logits, expo, probs, biased, rank, chosen = (prb[:, i] for i in range(6))

                def by_expert(col):
                    return col.unsqueeze(2).to_broadcast([P, G, NE])

                def bias(i):
                    return router_bias[:, i].unsqueeze(1).to_broadcast([P, G, NE])

                if due(1):
                    dve.wait_ge(s["logits_done"], g + 1)
                    nc.vector.tensor_tensor(logits, bank_out[:, 0:G * NE].rearrange("p (b e) -> p b e", b=G),
                                            bias(0), ALU.add).then_inc(s["r_step"], 1)
                if due(2):
                    nc.vector.reduce_max(red[:, 0], logits, AX_X).then_inc(s["r_step"], 1)
                if slot == AT["r_centred"]:
                    dve.wait_ge(s["r_step"], base + 2)
                    nc.vector.tensor_tensor(logits, logits, by_expert(red[:, 0]), ALU.subtract).then_inc(s["r_centred"], 1)
                if due(3):
                    dve.wait_ge(s["r_exp"], g + 1)
                    nc.vector.reduce_sum(red[:, 1], expo, AX_X).then_inc(s["r_step"], 1)
                if due(4):
                    nc.vector.reciprocal(red[:, 2], red[:, 1]).then_inc(s["r_step"], 1)
                if due(5):
                    nc.vector.tensor_tensor(probs, expo, by_expert(red[:, 2]), ALU.mult).then_inc(s["r_step"], 1)
                if due(6):
                    nc.vector.tensor_tensor(biased, probs, bias(1), ALU.add).then_inc(s["r_step"], 1)
                other = biased.unsqueeze(2).to_broadcast([P, G, NE, NE])
                own = biased.unsqueeze(3).to_broadcast([P, G, NE, NE])
                if due(7):
                    nc.vector.tensor_tensor(cmp_gt[:], other, own, ALU.is_gt).then_inc(s["r_step"], 1)
                if due(8):
                    nc.vector.tensor_tensor(cmp_eq[:], other, own, ALU.is_equal).then_inc(s["r_step"], 1)
                if due(9):
                    nc.vector.tensor_tensor(cmp_eq[:], cmp_eq[:], earlier[:].unsqueeze(1).to_broadcast([P, G, NE, NE]),
                                            ALU.mult).then_inc(s["r_step"], 1)
                if due(10):
                    nc.vector.tensor_tensor(cmp_gt[:], cmp_gt[:], cmp_eq[:], ALU.add).then_inc(s["r_step"], 1)
                if due(11):
                    nc.vector.reduce_sum(rank, cmp_gt[:], AX_X).then_inc(s["r_step"], 1)
                if due(12):
                    nc.vector.scalar_tensor_tensor(chosen, rank, float(TOP_K), probs, ALU.is_lt, ALU.mult).then_inc(s["r_step"], 1)
                if due(13):
                    nc.vector.reduce_sum(red[:, 3], chosen, AX_X).then_inc(s["r_step"], 1)
                if due(14):
                    nc.vector.reciprocal(red[:, 4], red[:, 3]).then_inc(s["r_step"], 1)
                if due(15):
                    nc.vector.tensor_scalar(red[:, 4], red[:, 4], half_gate[:], None, ALU.mult).then_inc(s["r_step"], 1)
                if due(16):
                    nc.vector.tensor_tensor(wgt[:], chosen, by_expert(red[:, 4]), ALU.mult).then_inc(s["r_step"], 1)
                if slot == AT["wgt_ready"]:
                    dve.wait_ge(s["r_step"], base + ROUTER_STEPS)
                    nc.vector.tensor_copy(wgt[:, :, NE - 1], half_gate[:].to_broadcast([P, G])).then_inc(s["wgt_ready"], 1)

            def expert_slot(g, slot):
                for e in range(NE):
                    if slot == min(3 * e + EXPERT_AT["acc_done"], SLOTS - 1):
                        dve.wait_ge(s["out_done"], NE * g + e + 1)
                        if e == 0:
                            dve.wait_ge(s["wgt_ready"], g + 1)
                            wait(dve, s["stored"], 16 * g)
                        else:
                            dve.wait_ge(s["acc_done"], NE * g + e)
                        for b in range(G):
                            last = nc.vector.scalar_tensor_tensor(acc[:, b], bank_out[:, b * D:(b + 1) * D], wgt[:, b, e:e + 1],
                                                                  (x23 if e == 0 else acc)[:, b], ALU.mult, ALU.add)
                        last.then_inc(s["acc_done"], 1)
                    if slot == 3 * e + EXPERT_AT["act_done"]:
                        dve.wait_ge(s["tanh_done"], NE * g + e + 1)
                        nc.vector.scalar_tensor_tensor(act_buf[:, e % 2], act_buf[:, e % 2], 1.0, bank_h1[e % 2][:],
                                                       ALU.add, ALU.mult).then_inc(s["act_done"], 1)
                    if slot == 3 * e + EXPERT_AT["gated_ready"]:
                        dve.wait_ge(s["h2_done"], NE * g + e + 1)
                        dve.wait_ge(s["act_done"], NE * g + e + 1)
                        nc.vector.tensor_tensor(act_buf[:, e % 2], act_buf[:, e % 2], bank_h2[e % 2][:],
                                                ALU.mult).then_inc(s["gated_ready"], 1)
                router(g, slot)

            def wkv_slot(g, slot):
                if slot == AT["stat0_done"]:
                    dve.wait_ge(s["ld_x"], 16 * (g + 1))
                    stats(xw, stat_w, 0)
                if slot == AT["mv0_done"]:
                    mean_var(stat_w, mv_w, 0, g + 1)
                if slot == AT["norm0_done"]:
                    dve.wait_ge(s["rstd0_done"], g + 1)
                    normalise(xwn, xw, mv_w, rstd_w, 0)
                if slot == AT["q_scanned"]:
                    dve.wait_ge(s["exp_done"], g + 1)
                    nc.vector.tensor_tensor_scan(q_state[:, 1:], flat3(decay[:]), flat3(ea[:]), 0.0, ALU.mult,
                                                 ALU.add).then_inc(s["q_scanned"], 1)
                if slot == AT["den_ready"]:
                    dve.wait_ge(s["q_scanned"], g + 1)
                    nc.vector.tensor_tensor(q_late, q_late, flat3(eb[:]), ALU.add).then_inc(s["den_ready"], 1)
                if slot == AT["eav_ready"]:
                    dve.wait_ge(s["ld_v"], 16 * C * (g + 1))
                    dve.wait_ge(s["q_scanned"], g + 1)
                    nc.vector.tensor_tensor(flat3(ea[:]), flat3(ea[:]), flat3(vT[:]), ALU.mult).then_inc(s["eav_ready"], 1)
                if slot == AT["p_scanned"]:
                    dve.wait_ge(s["eav_ready"], g + 1)
                    nc.vector.tensor_tensor_scan(p_state[:, 1:], flat3(decay[:]), flat3(ea[:]), 0.0, ALU.mult,
                                                 ALU.add).then_inc(s["p_scanned"], 1)
                parts = len(AT["den_inv"])
                for i in range(parts):
                    if slot == AT["den_inv"][i]:
                        dve.wait_ge(s["den_ready"], g + 1)
                        part = q_state[:, i * C * N // parts:(i + 1) * C * N // parts]
                        nc.vector.reciprocal(part, part).then_inc(s["den_inv"], 1)
                if slot == AT["y_raw"]:
                    dve.wait_ge(s["num_ready"], g + 1)
                    dve.wait_ge(s["den_inv"], parts * (g + 1))
                    nc.vector.tensor_tensor(flat3(ea[:]), p_late, q_late, ALU.mult).then_inc(s["y_raw"], 1)
                if slot == AT["y_ready"]:
                    dve.wait_ge(s["y_raw"], g + 1)
                    nc.vector.tensor_copy(ea[:, :, :, 0], vT[:, :, :, 0]).then_inc(s["y_ready"], 1)
                if slot == AT["x1_ready"]:
                    dve.wait_ge(s["ytr_done"], g + 1)
                    wait(dve, s["x2_ready"], g)
                    nc.vector.scalar_tensor_tensor(flat(x1[:]), side[1][:], gates[:, 0:1], flat(xw[:]), ALU.mult,
                                                   ALU.add).then_inc(s["x1_ready"], 1)
                if slot == AT["stat1_done"]:
                    dve.wait_ge(s["x1_ready"], g + 1)
                    stats(x1, stat_1, 1)
                if slot == AT["mv1_done"]:
                    mean_var(stat_1, mv_1, 1, g + 1)
                if slot == AT["norm1_done"]:
                    dve.wait_ge(s["rstd1_done"], g + 1)
                    wait(dve, s["ltr3_done"], g)
                    normalise(xfn, x1, mv_1, rstd_1, 1)
                if slot == AT["x1l_ready"]:
                    dve.wait_ge(s["x1h_ready"], g + 1)
                    split_lo(flat(xl[:]), side[2][:], flat(f32(xh[:])), s["x1l_ready"])

            def layer_slot(f, slot):
                if slot == AT["ffn_scaled"]:
                    dve.wait_ge(s["dn_done"], PAIRS * f + PAIRS)
                    wait(dve, s["acc_done"], NE * f - NE + 1)
                    nc.vector.tensor_tensor(x23[:], side[1][:].rearrange("p (b d) -> p b d", b=G),
                                            down_row[:].unsqueeze(1).to_broadcast([P, G, D]), ALU.mult).then_inc(s["ffn_scaled"], 1)
                if slot == AT["x2_ready"]:
                    dve.wait_ge(s["ffn_scaled"], f + 1)
                    nc.vector.tensor_tensor(x23[:], x23[:], x1[:], ALU.add).then_inc(s["x2_ready"], 1)
                if slot == AT["stat2_done"]:
                    dve.wait_ge(s["x2_ready"], f + 1)
                    stats(x23, stat_f, 2)
                if slot == AT["mv2_done"]:
                    mean_var(stat_f, mv_f, 2, f + 1)
                if slot == AT["norm2_done"]:
                    dve.wait_ge(s["rstd2_done"], f + 1)
                    normalise(xfn, x23, mv_f, rstd_f, 2)
                if slot == AT["x2l_ready"]:
                    dve.wait_ge(s["x2h_ready"], f + 1)
                    split_lo(flat(xl[:]), side[0][:], flat(f32(xh[:])), s["x2l_ready"])
                if slot == AT["ql_ready"]:
                    dve.wait_ge(s["qh_ready"], f + 1)
                    nc.vector.scalar_tensor_tensor(flat(ql), side[2][:], float(D) ** -0.5, flat(f32(qh)), ALU.mult,
                                                   ALU.subtract).then_inc(s["ql_ready"], 1)
                if slot == AT["kl_ready"]:
                    dve.wait_ge(s["kh_ready"], f + 1)
                    split_lo(flat3(kl[:, 1]), side[1][:], flat3(f32(kh[:, 1])), s["kl_ready"])
                if slot == AT["vl_ready"]:
                    dve.wait_ge(s["vh_ready"], f + 1)
                    split_lo(flat(vl[:, 1]), side[0][:], flat(f32(vh[:, 1])), s["vl_ready"])
                if slot == AT["max_ready"]:
                    dve.wait_ge(s["score_done"], f + 1)
                    nc.vector.reduce_max(row_max[:, 0], side[2][:].rearrange("p (b k) -> p b k", b=G), AX_X).then_inc(s["max_ready"], 1)
                if slot == AT["negmax_ready"]:
                    dve.wait_ge(s["max_ready"], f + 1)
                    nc.vector.tensor_scalar(row_max[:, 1], row_max[:, 0], -1.0, None, ALU.mult).then_inc(s["negmax_ready"], 1)
                if slot == AT["rowinv_ready"]:
                    dve.wait_ge(s["exp_p_done"], f + 1)
                    nc.vector.reciprocal(row_inv[:], row_sum[:]).then_inc(s["rowinv_ready"], 1)
                if slot == AT["ptl_ready"]:
                    dve.wait_ge(s["pth_ready"], f + 1)
                    split_lo(flat3(ptl), side[1][:], flat3(f32(pth)), s["ptl_ready"])
                if slot == AT["ol_ready"]:
                    dve.wait_ge(s["oh_ready"], f + 1)
                    split_lo(flat(ol), side[2][:], flat(f32(oh)), s["ol_ready"])
                if slot == AT["x3_ready"]:
                    dve.wait_ge(s["wo_done"], f + 1)
                    nc.vector.scalar_tensor_tensor(flat(x23[:]), side[1][:], gates[:, 1:2], flat(x23[:]), ALU.mult,
                                                   ALU.add).then_inc(s["x3_ready"], 1)
                if slot == AT["stat3_done"]:
                    dve.wait_ge(s["x3_ready"], f + 1)
                    stats(x23, stat_f, 3)
                if slot == AT["mv3_done"]:
                    mean_var(stat_f, mv_f, 3, f + 1)
                if slot == AT["norm3_done"]:
                    dve.wait_ge(s["rstd3_done"], f + 1)
                    normalise(xfn, x23, mv_f, rstd_f, 3)
                if slot == AT["xml_ready"]:
                    dve.wait_ge(s["xmh_ready"], f + 1)
                    split_lo(flat(xml[:]), side[0][:], flat(f32(xmh[:])), s["xml_ready"])

            def sign_piece(n):
                dve.wait_ge(landed[n % RING], 16 * (n // RING + 1))
                raw = work[:, n % RING]
                wait(dve, s["sign_done"], n)
                nc.vector.tensor_scalar(hid[:, 0], raw, 0.0, None, ALU.is_lt).then_inc(s["sign_neg"], 1)
                dve.wait_ge(s["sign_neg"], n + 1)
                nc.vector.scalar_tensor_tensor(signs[n], raw.rearrange("p (c n) -> p c n", c=2), 0.0,
                                               hid[:, 0].rearrange("p (c n) -> p c n", c=2), ALU.is_gt,
                                               ALU.subtract).then_inc(s["sign_done"], 1)

            def passage(g, experts, layer, wkv):
                for slot in range(SLOTS):
                    if experts:
                        expert_slot(g, slot)
                    if wkv:
                        wkv_slot(g + 2, slot)
                    if layer:
                        layer_slot(g + 1, slot)
                    if not experts and piece_of(layer, slot) < SIGNS:
                        sign_piece(piece_of(layer, slot))

            w_col, u_col = wu[:, 0], wu[:, 1]
            dve.wait_ge(s["ld_wu"], 32)
            nc.vector.tensor_scalar(chan[:, 5], w_col, 0.0, None, ALU.min).then_inc(s["chan_step"], 1)
            dve.wait_ge(s["chan_step"], 2)
            nc.vector.tensor_scalar(chan[:, 0], w_col, 0.0, None, ALU.max).then_inc(s["chan_step"], 1)
            dve.wait_ge(s["chan_step"], 3)
            nc.vector.tensor_scalar(chan[:, 1], chan[:, 0], -1.0, None, ALU.mult).then_inc(s["chan_step"], 1)
            dve.wait_ge(s["chan_step"], 4)
            nc.vector.tensor_tensor(chan[:, 2], chan[:, 1], u_col, ALU.max).then_inc(s["chan_step"], 1)
            dve.wait_ge(s["chan_step"], 5)
            nc.vector.tensor_tensor(chan[:, 3], chan[:, 1], chan[:, 2], ALU.subtract).then_inc(s["chan_step"], 1)
            nc.vector.tensor_tensor(chan[:, 4], u_col, chan[:, 2], ALU.subtract).then_inc(s["chan_step"], 1)
            dve.wait_ge(s["ld_ramp"], 16)
            dve.wait_ge(s["consts_pool"], 5)
            nc.vector.tensor_scalar(ramp[:], ramp[:], 0.0, time_col[:], ALU.max, ALU.mult).then_inc(s["ramp_ready"], 1)
            nc.vector.memset(decay[:], 1.0).then_inc(s["decay_step"], 1)
            dve.wait_ge(s["decay_step"], 1)
            for c in range(C):
                last = nc.vector.tensor_scalar(flat(decay[:, c]), flat(decay[:, c]), chan[:, 5, c:c + 1], None, ALU.mult)
            last.then_inc(s["decay_step"], 1)
            dve.wait_ge(s["decay_step"], 2)
            nc.vector.memset(decay[:, :, :, 0], 0.0).then_inc(s["decay_step"], 1)
            nc.vector.memset(q_state[:, 0:1], 1.0).then_inc(s["decay_step"], 1)
            dve.wait_ge(s["decay_step"], 4)
            dve.wait_ge(s["gates_ready"], 1)
            nc.vector.tensor_scalar(half_gate[:], gates[:, 3:4], 0.5, None, ALU.mult).then_inc(s["scales_ready"], 1)
            dve.wait_ge(s["ld_drow"], 16)
            nc.vector.tensor_scalar(down_row[:], down_row[:], gates_raw[:, 4:5], gates[:, 2:3], ALU.mult,
                                    ALU.mult).then_inc(s["scales_ready"], 1)
            dve.wait_ge(s["scales_ready"], 2)
            passage(-2, False, False, True)
            dve.wait_ge(s["ld_rbias"], 32)
            passage(-1, False, True, True)
            passage(0, True, True, True)
            with dve.Fori(1, NG - 2) as g:
                passage(g, True, True, True)
            passage(NG - 2, True, True, False)
            passage(NG - 1, True, False, False)


def kernel(**inputs):
    import numpy as _np
    import concourse.bacc as _bacc
    from concourse import mybir as _mybir
    from concourse.bass_utils import run_bass_kernel_spmd as _run

    layout = [
        ("x", inputs["x"]),
        ("ctx_in", inputs["ctx_2048"]),
        ("ctxT_in", _np.transpose(inputs["ctx_2048"], (0, 2, 1))),
        ("g_xattn", inputs["g_xattn"]), ("g_ffn", inputs["g_ffn"]),
        ("w_in", inputs["L0_xattn_w"]),
        ("w_cols", _np.transpose(inputs["L0_xattn_w"].reshape(-1, P))),
        ("u_cols", _np.transpose(inputs["L0_xattn_u"].reshape(-1, P))),
        ("upT_in", _np.transpose(inputs["L0_ffn_up_weight"])),
        ("downT_in", _np.transpose(inputs["L0_ffn_down_weight"])),
        ("up_cols", _np.transpose(inputs["L0_ffn_up_scale"].reshape(-1, P))),
         ("down_scale", inputs["L0_ffn_down_scale"]),
        ("output_scale", inputs["L0_ffn_output_scale"]),
        ("wqT_in", _np.transpose(inputs["L1_xattn_wq"])), ("wkT_in", _np.transpose(inputs["L1_xattn_wk"])),
        ("wvT_in", _np.transpose(inputs["L1_xattn_wv"])), ("woT_in", _np.transpose(inputs["L1_xattn_wo"])),
        ("W1", inputs["L1_ffn_W1"]), ("Wg", inputs["L1_ffn_Wg"]), ("W2", inputs["L1_ffn_W2"]),
        ("Ws1", inputs["L1_ffn_Ws1"]), ("Wsg", inputs["L1_ffn_Wsg"]), ("Ws2", inputs["L1_ffn_Ws2"]),
        ("gate_w", inputs["L1_ffn_gate_w"]), ("gate_b", inputs["L1_ffn_gate_b"]), ("biases", inputs["L1_ffn_biases"]),
    ]
    nc = _bacc.Bacc("TRN2", target_bir_lowering=False, num_devices=1)
    arrays, args = {}, {}
    for name, a in layout:
        a = _np.ascontiguousarray(a)
        arrays[f"in_{name}"] = a
        args[name] = nc.dram_tensor(f"in_{name}", a.shape, _mybir.dt.from_np(a.dtype), kind="ExternalInput").ap()
    args["out"] = nc.dram_tensor("out_0", inputs["x"].shape, _mybir.dt.float32, kind="ExternalOutput").ap()
    flamingo_kernel(nc, **args)
    return _run(nc, [arrays], core_ids=[0]).results[0]["out_0"]
```

```python
import concourse.bass as bass
from concourse import mybir
from contextlib import ExitStack

F32 = mybir.dt.float32
F32R = mybir.dt.float32r
ALU = mybir.AluOpType
ACT = mybir.ActivationFunctionType
AX_X = mybir.AxisListType.X

P = 128
EPS = 1e-5
NEVER = -1e30
TOP_K = 3
SLOTS = 25
RING = 7
ROUTER_STEPS = 16

AT = {
    "ktr_done": 4, "ytr_done": 15, "ltr1_done": 20,
    "exp_done": 3, "x1h_ready": 19,
    "stat0_done": 0, "mv0_done": 0, "norm0_done": 1, "q_scanned": 2, "den_ready": 4, "eav_ready": 8,
    "p_scanned": 9, "den_inv": (5, 10, 6, 10), "y_raw": 11, "y_ready": 12, "x1_ready": 14, "stat1_done": 14,
    "mv1_done": 15, "norm1_done": 17, "x1l_ready": 21,
    "var0_done": 0, "rstd0_done": 0, "ramp_added": 0, "ebv_ready": 7, "num_ready": 10, "var1_done": 13,
    "rstd1_done": 16,
    "up_done": (23, 2, 4, 6), "dn_done": (1, 5, 7, 8), "ltr2_done": 12, "q_done": 13, "k_done": 13,
    "v_done": 14, "score_done": 14, "ptr_done": 16, "pv_done": 17, "otr_done": 18, "wo_done": 19,
    "ltr3_done": 23,
    "hid_ready": (23, 2, 3, 4), "hid_hi_ready": (24, 2, 3, 5), "x2h_ready": 8, "qh_ready": 9, "kh_ready": 11,
    "vh_ready": 13, "kc_hi": 3, "vc_hi": 0, "exp_p_done": 13, "pth_ready": 13, "att_scaled": 16, "oh_ready": 16,
    "xmh_ready": 23,
    "ffn_scaled": 6, "x2_ready": 6, "stat2_done": 6, "mv2_done": 6, "norm2_done": 7, "x2l_ready": 9,
    "ql_ready": 10, "kl_ready": 11, "vl_ready": 15, "max_ready": 13, "negmax_ready": 13, "rowinv_ready": 14,
    "ptl_ready": 15, "ol_ready": 18, "x3_ready": 19, "stat3_done": 19, "mv3_done": 19, "norm3_done": 22,
    "xml_ready": 23,
    "hid_lo_ready": (24, 1, 3, 3), "var2_done": 5, "rstd2_done": 6, "kc_lo": 4, "vc_lo": 6, "var3_done": 21,
    "rstd3_done": 22,
    "logits_out": 2, "r_exp": 3,
    "r_step": (2, 2, 2, 2, 2, 2, 2, 2, 2, 2, 3, 4, 5, 5, 5, 5), "r_centred": 2, "wgt_ready": 5,
}
EXPERT_AT = {"tanh_done": 0, "act_done": 1, "gated_ready": 1, "ghi_ready": 2, "glo_ready": 2}
OUT_AT = (7, 11, 14, 17, 19, 21, 23, 24)
ACC_AT = (6, 9, 14, 16, 19, 20, 23, 24)
START_AT = {
    "ktr_done": 12, "ytr_done": 17, "ltr1_done": 24,
    "exp_done": 7, "x1h_ready": 22,
    "stat0_done": 0, "mv0_done": 0, "norm0_done": 2, "q_scanned": 8, "den_ready": 9, "eav_ready": 10,
    "p_scanned": 12, "den_inv": (12, 10, 15, 12), "y_raw": 17, "y_ready": 17, "x1_ready": 18, "stat1_done": 18,
    "mv1_done": 21, "norm1_done": 22, "x1l_ready": 24,
    "var0_done": 0, "rstd0_done": 0, "ramp_added": 2, "ebv_ready": 8, "num_ready": 11, "var1_done": 14,
    "rstd1_done": 15,
    "up_done": (24, 0, 1, 2), "dn_done": (2, 3, 4, 6), "ltr2_done": 12, "q_done": 13, "k_done": 13,
    "v_done": 17, "score_done": 15, "ptr_done": 17, "pv_done": 18, "otr_done": 18, "wo_done": 18,
    "ltr3_done": 24,
    "hid_ready": (24, 0, 0, 1), "hid_hi_ready": (24, 0, 0, 4), "x2h_ready": 7, "qh_ready": 10, "kh_ready": 10,
    "vh_ready": 12, "kc_hi": 0, "vc_hi": 6, "exp_p_done": 10, "pth_ready": 13, "att_scaled": 16, "oh_ready": 19,
    "xmh_ready": 22,
    "ffn_scaled": 4, "x2_ready": 4, "stat2_done": 4, "mv2_done": 7, "norm2_done": 8, "x2l_ready": 10,
    "ql_ready": 14, "kl_ready": 15, "vl_ready": 21, "max_ready": 17, "negmax_ready": 17, "rowinv_ready": 21,
    "ptl_ready": 21, "ol_ready": 21, "x3_ready": 22, "stat3_done": 22, "mv3_done": 22, "norm3_done": 24,
    "xml_ready": 24,
    "hid_lo_ready": (24, 0, 0, 1), "var2_done": 5, "rstd2_done": 6, "kc_lo": 3, "vc_lo": 8, "var3_done": 21,
    "rstd3_done": 21,
}
SIGN_AT = (0, 4, 5, 17, 21, 22, 24, 24)
HI_AT = (13, 13, 17, 22, 23, 25, 25, 29, 29, 29, 29, 29, 30, 32, 33, 34, 34, 40, 40, 40, 43, 44, 44, 44, 44, 44, 45, 48)
LO_AT = (12, 15, 18, 22, 23, 25, 28, 31, 32, 32, 36, 36, 37, 37, 37, 37, 39, 39, 39, 39, 40, 44, 45, 45, 46, 47, 47, 48)
BEFORE_X = 11
SCAN_CONSTANTS_AT = 5


def flamingo_kernel(nc, x, ctx_in, ctxT_in, g_xattn, g_ffn, w_in, w_cols, u_cols, upT_in, downT_in, up_cols,
                    down_scale, output_scale, wqT_in, wkT_in, wvT_in, woT_in, W1, Wg, W2, Ws1, Wsg,
                    Ws2, gate_w, gate_b, biases, out):
    B, T, D = x.shape
    C = D // P
    H = upT_in.shape[1]
    M = H // P
    NE = W1.shape[0] + 1
    NR = W1.shape[0]
    G = 2
    NG = B // G
    N = G * T
    PAIRS = M // 2
    assert T == P and C == 2 and NE == 8 and N * 2 == 512

    ctx = ExitStack()
    with ctx:
        def sb(name, shape, dt=F32):
            return ctx.enter_context(nc.sbuf_tensor(name, shape, dt))

        def bank(name):
            return ctx.enter_context(nc.psum_tensor(name, [P, 512], F32))

        def f32(ap):
            return ap.bitcast(F32)

        def flat(ap):
            return ap.rearrange("p a b -> p (a b)")

        def flat3(ap):
            return ap.rearrange("p a b c -> p (a b c)")

        bank_h1 = [bank("h1_0"), bank("h1_1")]
        bank_h2 = [bank("h2_0"), bank("h2_1")]
        bank_out = bank("expert_out")
        side = [bank(f"side{i}") for i in range(3)]

        moe_hi = sb("moe_hi", [P, NE, 3, C, D], F32R)
        moe_lo = sb("moe_lo", [P, NE, 3, C, D], F32R)
        up_sign = sb("up_sign", [P, C, H], F32R)
        down_sign = sb("down_sign", [P, M, D], F32R)
        att_hi = sb("att_hi", [P, 4, C, D], F32R)
        att_lo = sb("att_lo", [P, 4, C, D], F32R)
        gate_raw = sb("gate_raw", [P, C, NE])
        gate_hi = sb("gate_hi", [P, C, NE], F32R)
        gate_lo = sb("gate_lo", [P, C, NE], F32R)

        ident = sb("ident", [P, P])
        wu = sb("wu", [P, 2, C])
        chan = sb("chan", [P, 6, C])
        decay = sb("decay", [P, C, G, T])
        ramp = sb("ramp", [P, D])
        time_col = sb("time_col", [P, 1])
        gates_raw = sb("gates_raw", [P, 5])
        gates = sb("gates", [P, 4])
        half_gate = sb("half_gate", [P, 1])
        down_row = sb("down_row", [P, D])
        up_col = sb("up_col", [P, M])
        router_bias = sb("router_bias", [P, 2, NE])
        earlier = sb("earlier", [P, NE, NE])
        minus_half = sb("minus_half", [P, G])
        eps = sb("eps", [P, G])
        scratch = sb("scratch", [P, 1])

        xw = sb("xw", [P, G, D])
        vT = sb("vT", [P, C, G, T])
        ea = sb("ea", [P, C, G, T])
        eb = sb("eb", [P, C, G, T])
        p_state = sb("p_state", [P, 1 + C * N])
        q_state = sb("q_state", [P, 1 + C * N])
        p_late, q_late = p_state[:, 0:C * N], q_state[:, 0:C * N]
        xwn = p_late.rearrange("p (b d) -> p b d", b=G)
        stat_w = sb("stat_w", [P, G, 6])
        mv_w = sb("mv_w", [P, G, 2])
        rstd_w = sb("rstd_w", [P, 2, G])
        x1 = sb("x1", [P, G, D])
        stat_1 = sb("stat_1", [P, G, 6])
        mv_1 = sb("mv_1", [P, G, 2])
        rstd_1 = sb("rstd_1", [P, 2, G])
        x23 = sb("x23", [P, G, D])
        x1n = flat3(ea[:]).rearrange("p (b d) -> p b d", b=G)
        xfn = sb("xfn", [P, G, D])
        att = xfn
        stat_f = sb("stat_f", [P, G, 6])
        mv_f = sb("mv_f", [P, G, 2])
        rstd_f = sb("rstd_f", [P, 2, G])
        xh = sb("xh", [P, C, N], F32R)
        xl = sb("xl", [P, C, N], F32R)
        pth = xh[:].rearrange("p k (b t) -> p k b t", b=G)
        ptl = xl[:].rearrange("p k (b t) -> p k b t", b=G)
        hid = sb("hid", [P, 2, 2 * N])
        prob = hid[:, 0].rearrange("p (b k t) -> p b k t", b=G, k=2)
        hid_hi = sb("hid_hi", [P, 2, 2, N], F32R)
        hid_lo = sb("hid_lo", [P, 2, 2, N], F32R)
        qh, ql = hid_hi[:, 0], hid_lo[:, 0]
        oh, ol = hid_hi[:, 1], hid_lo[:, 1]
        ctxT_a = sb("ctxT_a", [P, C, G, T])
        ctx_a = sb("ctx_a", [P, G, D])
        kh = sb("kh", [P, 2, C, G, T], F32R)
        kl = sb("kl", [P, 2, C, G, T], F32R)
        vh = sb("vh", [P, 2, G, D], F32R)
        vl = sb("vl", [P, 2, G, D], F32R)
        row_max = sb("row_max", [P, 2, G])
        row_sum = sb("row_sum", [P, G])
        row_inv = sb("row_inv", [P, G])
        xmh = sb("xmh", [P, C, N], F32R)
        xml = sb("xml", [P, C, N], F32R)
        work = sb("work", [P, 3, C * N])
        act_buf = work[:, 0:2]
        acc = work[:, 2].rearrange("p (b d) -> p b d", b=G)
        with nc.sbuf_tensor("more_raw", [P, RING - 3, C * N], F32) as more_raw:
            pass
        gated_hi = sb("gated_hi", [P, 2, C, N], F32R)
        gated_lo = sb("gated_lo", [P, 2, C, N], F32R)
        prb = sb("prb", [P, 6, G, NE])
        cmp = sb("cmp", [P, 2, G, NE, NE])
        cmp_gt, cmp_eq = cmp[:, 0], cmp[:, 1]
        logitsT = cmp[0:NE].rearrange("p a b c d -> p (a b c d)")
        assert 2 * G * NE * NE == N
        red = sb("red", [P, 5, G])
        wgt = sb("wgt", [P, G, NE])

        pieces = [upT_in.rearrange("(c p) h -> p c h", p=P)[:, :, j * D:(j + 1) * D] for j in range(H // D)]
        pieces += [downT_in.rearrange("(m p) d -> p m d", p=P)[:, 2 * j:2 * j + 2, :] for j in range(M // 2)]
        SIGNS = len(pieces)
        signs = [up_sign[:, :, j * D:(j + 1) * D] for j in range(H // D)]
        signs += [down_sign[:, 2 * j:2 * j + 2, :] for j in range(M // 2)]
        pieces += [w.rearrange("(c p) n -> p c n", p=P) for w in (wqT_in, wkT_in, wvT_in, woT_in)]
        splits = [(att_hi[:, i], att_lo[:, i]) for i in range(4)]
        LAYER_PIECES = len(pieces)
        for e in range(NE):
            for i, w in enumerate((W1[e], Wg[e], W2[e]) if e < NR else (Ws1, Wsg, Ws2)):
                pieces.append(w.rearrange("(c p) n -> p c n", p=P))
                splits.append((moe_hi[:, e, i], moe_lo[:, e, i]))

        names = """
        ld_x ld_v ld_ctxT ld_ctx ld_wu ld_ramp ld_gates ld_upcol ld_drow ld_gatew ld_rbias
        ld_piece0 ld_piece1 ld_piece2 ld_piece3 ld_piece4 ld_piece5 ld_piece6 stored
        ident_ready consts_pool bias_fill chan_step decay_step ramp_ready gates_ready scales_ready
        gate_hi_ready gate_lo_ready sign_neg sign_done split_hi_done split_lo_done
        stat0_done mv0_done var0_done rstd0_done norm0_done ramp_added ktr_done exp_done
        q_scanned den_ready den_inv eav_ready p_scanned ebv_ready num_ready y_raw y_ready ytr_done x1_ready
        stat1_done mv1_done var1_done rstd1_done norm1_done ltr1_done x1h_ready x1l_ready
        stat2_done mv2_done var2_done rstd2_done norm2_done ltr2_done x2h_ready x2l_ready
        stat3_done mv3_done var3_done rstd3_done norm3_done ltr3_done up_done hid_ready hid_hi_ready hid_lo_ready
        dn_done ffn_scaled x2_ready kc_hi kc_lo vc_hi vc_lo q_done k_done v_done qh_ready ql_ready kh_ready
        kl_ready vh_ready vl_ready score_done max_ready negmax_ready exp_p_done rowinv_ready ptr_done
        pth_ready ptl_ready pv_done att_scaled otr_done oh_ready ol_ready wo_done x3_ready
        xmh_ready xml_ready
        h1_done tanh_done act_done h2_done gated_ready ghi_ready glo_ready out_done acc_done
        logits_done logits_out logits_turned r_step r_centred r_exp wgt_ready
        """.split()
        s = {n: ctx.enter_context(nc.semaphore(n)) for n in names}

        def wait(eng, sem, value):
            if not (isinstance(value, int) and value <= 0):
                eng.wait_ge(sem, value)

        x_g = x.rearrange("(g b) t d -> t (g b) d", b=G)
        out_g = out.rearrange("(g b) t d -> t (g b) d", b=G)
        ctx_g = ctx_in.rearrange("(g b) t d -> t (g b) d", b=G)
        ctxT_g = ctxT_in.rearrange("(g b) (c p) t -> p c (g b) t", b=G, p=P)

        def expert_at(step, e):
            return min(3 * e + EXPERT_AT[step], SLOTS - 1)

        def hidden_bank(f, p):
            return (bank_h1 + bank_h2)[p] if isinstance(f, int) and f == 0 else side[2]

        def group(g):
            return bass.ds(g * G, G)

        def pieces_of(table, layer, slot):
            return [n for n, at in enumerate(table) if at == slot + (SLOTS if layer else 0)]

        ring = [buf.rearrange("p (c n) -> p c n", c=2) for buf in
                (more_raw[:, 3], work[:, 0], work[:, 1], more_raw[:, 0], more_raw[:, 2], work[:, 2], more_raw[:, 1])]
        first_use = ("act_buf 0", "act_buf 1", "gated_hi 0", "gated_lo 0", "acc", "gated_hi 1", "gated_lo 1")
        raw_out = {buf: len(splits) - RING + 1 + i for i, buf in enumerate(first_use)}
        assert (len(pieces) - RING) % RING == 1
        landed = [s[f"ld_piece{i}"] for i in range(RING)]

        block = ctx.enter_context(nc.Block())

        @block.sync
        def _(sp):
            def load_wkv(g):
                for c in range(C):
                    sp.dma_start(vT[:, c], ctxT_g[:, c, group(g), :]).then_inc(s["ld_v"], 16)
                sp.dma_start(xw[:], x_g[:, group(g), :]).then_inc(s["ld_x"], 16)

            def load_ctx(g):
                for c in range(C):
                    sp.dma_start(ctxT_a[:, c], ctxT_g[:, c, group(g), :]).then_inc(s["ld_ctxT"], 16)
                sp.dma_start(ctx_a[:], ctx_g[:, group(g), :]).then_inc(s["ld_ctx"], 16)

            def next_ctx(f):
                sp.wait_ge(s["kc_lo"], f + 1)
                sp.wait_ge(s["vc_lo"], f + 1)
                load_ctx(f + 1)

            def next_wkv(g):
                sp.wait_ge(s["x1_ready"], g + 1)
                load_wkv(g + 1)

            def store(g):
                sp.wait_ge(s["acc_done"], NE * g + NE)
                sp.dma_start(out_g[:, group(g), :], acc[:]).then_inc(s["stored"], 16)

            def load_piece(n):
                if n >= RING:
                    if n - RING < SIGNS:
                        sp.wait_ge(s["sign_done"], n - RING + 1)
                    else:
                        sp.wait_ge(s["split_lo_done"], n - RING - SIGNS + 1)
                sp.dma_start(ring[n % RING], pieces[n]).then_inc(landed[n % RING], 16)

            sp.dma_start(xw[:], x_g[:, group(0), :]).then_inc(s["ld_x"], 16)
            sp.dma_start(wu[:, 0], w_cols).then_inc(s["ld_wu"], 16)
            sp.dma_start(wu[:, 1], u_cols).then_inc(s["ld_wu"], 16)
            sp.dma_start(ramp[:], w_in.rearrange("(a d) -> a d", a=1).to_broadcast([P, D])).then_inc(s["ld_ramp"], 16)
            for c in range(C):
                sp.dma_start(vT[:, c], ctxT_g[:, c, group(0), :]).then_inc(s["ld_v"], 16)
            for n in range(3):
                load_piece(n)
            for i, g in enumerate((g_xattn, g_ffn)):
                sp.dma_start(gates_raw[:, 2 * i:2 * i + 2],
                             g.rearrange("(a d) -> a d", a=1).to_broadcast([P, 2])).then_inc(s["ld_gates"], 16)
            sp.dma_start(gates_raw[:, 4:5],
                         output_scale.rearrange("(a d) -> a d", a=1).to_broadcast([P, 1])).then_inc(s["ld_gates"], 16)
            sp.dma_start(down_row[:], down_scale.rearrange("(a d) -> a d", a=1).to_broadcast([P, D])).then_inc(s["ld_drow"], 16)
            sp.dma_start(up_col[:], up_cols).then_inc(s["ld_upcol"], 16)
            load_ctx(0)
            sp.wait_ge(s["bias_fill"], 2)
            for i, r in enumerate((gate_b, biases)):
                sp.dma_start(router_bias[:, i, 0:NR],
                             r.rearrange("(a d) -> a d", a=1).to_broadcast([P, NR])).then_inc(s["ld_rbias"], 16)
            sp.dma_start(gate_raw[:, :, 0:NR], gate_w.rearrange("(c p) e -> p c e", p=P)).then_inc(s["ld_gatew"], 16)
            for n in range(3, BEFORE_X):
                load_piece(n)
            next_wkv(0)
            for n in range(BEFORE_X, len(pieces)):
                load_piece(n)
            next_ctx(0)
            next_wkv(1)
            with sp.Fori(0, NG - 3) as g:
                next_ctx(g + 1)
                next_wkv(g + 2)
                store(g)
            next_ctx(NG - 2)
            for g in range(NG - 3, NG):
                store(g)
            sp.wait_ge(s["stored"], 16 * NG)

        @block.tensor
        def _(pe):
            def transpose8(dst, src):
                for c in range(C):
                    for b in range(G):
                        last = nc.tensor.transpose(dst[:, (c * G + b) * P:(c * G + b + 1) * P],
                                                   src[:, b, c * P:(c + 1) * P], ident[:])
                return last

            def accumulate(steps, part, parts):
                for i, (dst, a, b) in enumerate(steps):
                    last = nc.tensor.matmul(dst, a, b, start=(part == 0 and i == 0),
                                            stop=(part == parts - 1 and i == len(steps) - 1), skip_group_check=True)
                return last

            def weights_by_tokens(dst, hi, lo, mh, ml, lo_ready=None):
                def steps(w, m):
                    return [(dst[:, n * N:(n + 1) * N], w[:, d, n * P:(n + 1) * P], m[:, d]) for n in range(2) for d in range(C)]
                accumulate(steps(hi, mh) + steps(lo, mh), 0, 2)
                if lo_ready:
                    pe.wait_ge(*lo_ready)
                return accumulate(steps(hi, ml), 1, 2)

            def tokens_by_weights(dst, mh, ml, hi, lo, lo_ready=None):
                def steps(m, w):
                    return [(dst[:, b * D:(b + 1) * D], m[:, d, b * P:(b + 1) * P], w[:, d]) for b in range(G) for d in range(C)]
                accumulate(steps(mh, hi) + steps(mh, lo), 0, 2)
                if lo_ready:
                    pe.wait_ge(*lo_ready)
                return accumulate(steps(ml, hi), 1, 2)

            def expert_weights(g, e, count):
                if isinstance(g, int) and g == 0:
                    pe.wait_ge(s["split_lo_done"], LAYER_PIECES - SIGNS + 3 * e + count)

            def expert_slot(g, slot):
                for d in [d for d in range(NE) if slot == OUT_AT[d]]:
                    expert_weights(g, d, 3)
                    pe.wait_ge(s["ghi_ready"], NE * g + d + 1)
                    if d == 0:
                        pe.wait_ge(s["r_step"], ROUTER_STEPS * g + 1)
                    else:
                        pe.wait_ge(s["acc_done"], NE * g + d)
                    tokens_by_weights(bank_out, gated_hi[:, d % 2], gated_lo[:, d % 2],
                                      moe_hi[:, d, 2], moe_lo[:, d, 2],
                                      (s["glo_ready"], NE * g + d + 1)).then_inc(s["out_done"], 1)
                e, part = divmod(slot, 3)
                if slot < 3 * NE and part == 0:
                    expert_weights(g, e, 1)
                    if e == 0:
                        pe.wait_ge(s["xmh_ready"], g + 1)
                    wait(pe, s["act_done"], NE * g + e - 1)
                    if e == 1:
                        pe.wait_ge(s["logits_out"], g + 1)
                    weights_by_tokens(bank_h1[e % 2], moe_hi[:, e, 0], moe_lo[:, e, 0], xmh, xml,
                                      (s["xml_ready"], g + 1) if e == 0 else None).then_inc(s["h1_done"], 1)
                    if e == 1:
                        for b in range(G):
                            last = nc.tensor.transpose(bank_out[:, b * NE:(b + 1) * NE], logitsT[:, b * P:(b + 1) * P],
                                                       ident[0:NE, 0:NE])
                        last.then_inc(s["logits_turned"], 1)
                if slot < 3 * NE and part == 1:
                    expert_weights(g, e, 2)
                    wait(pe, s["gated_ready"], NE * g + e - 1)
                    weights_by_tokens(bank_h2[e % 2], moe_hi[:, e, 1], moe_lo[:, e, 1], xmh, xml).then_inc(s["h2_done"], 1)
                    if slot == 1:
                        wait(pe, s["acc_done"], NE * g)
                        last = accumulate([(bank_out[0:NE, 0:N], w[:, d], m[:, d]) for d in range(C)
                                           for w, m in ((gate_hi, xmh), (gate_lo, xmh), (gate_hi, xml))], 0, 1)
                        last.then_inc(s["logits_done"], 1)

            def up(f, p):
                if isinstance(f, int) and f == 0:
                    pe.wait_ge(s["sign_done"], p + 1)
                if p == 0:
                    pe.wait_ge(s["x1h_ready"], f + 1)
                elif not (isinstance(f, int) and f == 0):
                    pe.wait_ge(s["hid_ready"], PAIRS * f + p)
                for i, part in enumerate((xh, xl)):
                    if p == 0 and i == (1 if isinstance(f, int) and f == 0 else 0):
                        pe.wait_ge(s["x1l_ready"], f + 1)
                    last = accumulate([(hidden_bank(f, p)[:, k * N:(k + 1) * N],
                                        up_sign[:, d, (2 * p + k) * P:(2 * p + k + 1) * P], part[:, d])
                                       for k in range(2) for d in range(C)], i, 2)
                last.then_inc(s["up_done"], 1)

            def wkv_slot(g, slot, at):
                if slot == at["ktr_done"]:
                    pe.wait_ge(s["ramp_added"], g + 1)
                    wait(pe, s["xmh_ready"], g - 1)
                    wait(pe, s["xml_ready"], g - 1)
                    transpose8(side[0], xwn).then_inc(s["ktr_done"], 1)
                if slot == at["ytr_done"]:
                    pe.wait_ge(s["y_ready"], g + 1)
                    wait(pe, s["kh_ready"], g)
                    wait(pe, s["kl_ready"], g)
                    for b in range(G):
                        for c in range(C):
                            last = nc.tensor.transpose(side[1][:, b * D + c * P:b * D + (c + 1) * P],
                                                       ea[:, c, b], ident[:])
                    last.then_inc(s["ytr_done"], 1)
                if slot == at["ltr1_done"]:
                    pe.wait_ge(s["norm1_done"], g + 1)
                    wait(pe, s["ol_ready"], g)
                    transpose8(side[2], x1n).then_inc(s["ltr1_done"], 1)
                if slot == at["up_done"][0]:
                    up(g, 0)

            def attention_weights(f, count):
                if isinstance(f, int) and f == 0:
                    pe.wait_ge(s["split_lo_done"], count)

            def layer_slot(f, slot, at, beside_wkv):
                for p in range(PAIRS):
                    if p > 0 and slot == at["up_done"][p]:
                        up(f, p)
                    if slot == at["dn_done"][p]:
                        if isinstance(f, int) and f == 0:
                            pe.wait_ge(s["sign_done"], PAIRS + p + 1)
                        if p == 0:
                            wait(pe, s["x3_ready"], f)
                        for i, (part, ready) in enumerate(((hid_hi, s["hid_hi_ready"]), (hid_lo, s["hid_lo_ready"]))):
                            pe.wait_ge(ready, PAIRS * f + p + 1)
                            last = accumulate([(side[1][:, b * D:(b + 1) * D], part[:, p % 2, k, b * P:(b + 1) * P],
                                                down_sign[:, 2 * p + k]) for k in range(2) for b in range(G)],
                                              2 * p + i, 2 * PAIRS)
                        last.then_inc(s["dn_done"], 1)
                if slot == at["ltr2_done"]:
                    pe.wait_ge(s["norm2_done"], f + 1)
                    if beside_wkv:
                        pe.wait_ge(s["exp_done"], f + 2)
                    transpose8(side[0], xfn).then_inc(s["ltr2_done"], 1)
                if slot == at["q_done"]:
                    attention_weights(f, 1)
                    pe.wait_ge(s["x2h_ready"], f + 1)
                    weights_by_tokens(side[2], att_hi[:, 0], att_lo[:, 0], xh, xl, (s["x2l_ready"], f + 1)).then_inc(s["q_done"], 1)
                if slot == at["k_done"]:
                    attention_weights(f, 2)
                    weights_by_tokens(side[1], att_hi[:, 1], att_lo[:, 1], xh, xl).then_inc(s["k_done"], 1)
                if slot == at["v_done"]:
                    attention_weights(f, 3)
                    tokens_by_weights(side[0], xh, xl, att_hi[:, 2], att_lo[:, 2]).then_inc(s["v_done"], 1)
                if slot == at["score_done"]:
                    for ready in (s["qh_ready"], s["ql_ready"], s["kh_ready"]):
                        pe.wait_ge(ready, f + 1)
                    for i, (query, keys) in enumerate(((qh, kh), (ql, kh), (qh, kl))):
                        if i == 2:
                            pe.wait_ge(s["kl_ready"], f + 1)
                            pe.wait_ge(s["kc_lo"], f + 1)
                        last = accumulate([(side[2][:, b * 2 * T:(b + 1) * 2 * T], query[:, c, b * P:(b + 1) * P],
                                            keys[:, :, c, b]) for b in range(G) for c in range(C)], i, 3)
                    last.then_inc(s["score_done"], 1)
                if slot == at["ptr_done"]:
                    pe.wait_ge(s["exp_p_done"], f + 1)
                    if beside_wkv:
                        pe.wait_ge(s["x1_ready"], f + 2)
                    for part in range(2):
                        for b in range(G):
                            last = nc.tensor.transpose(side[1][:, (part * G + b) * P:(part * G + b + 1) * P],
                                                       prob[:, b, part], ident[:])
                    last.then_inc(s["ptr_done"], 1)
                if slot == at["pv_done"]:
                    for ready in (s["pth_ready"], s["vh_ready"], s["vl_ready"], s["vc_lo"]):
                        pe.wait_ge(ready, f + 1)
                    for i, (weights, values) in enumerate(((pth, vh), (pth, vl), (ptl, vh))):
                        if i == 2:
                            pe.wait_ge(s["ptl_ready"], f + 1)
                        last = accumulate([(side[0][:, b * D:(b + 1) * D], weights[:, part, b], values[:, part, b])
                                           for b in range(G) for part in range(2)], i, 3)
                    last.then_inc(s["pv_done"], 1)
                if slot == at["otr_done"]:
                    pe.wait_ge(s["att_scaled"], f + 1)
                    transpose8(side[2], att).then_inc(s["otr_done"], 1)
                if slot == at["wo_done"]:
                    attention_weights(f, 4)
                    pe.wait_ge(s["oh_ready"], f + 1)
                    tokens_by_weights(side[1], oh, ol, att_hi[:, 3], att_lo[:, 3], (s["ol_ready"], f + 1)).then_inc(s["wo_done"], 1)
                if slot == at["ltr3_done"]:
                    pe.wait_ge(s["norm3_done"], f + 1)
                    transpose8(side[0], xfn).then_inc(s["ltr3_done"], 1)

            def passage(g, experts, layer, wkv):
                at = AT if experts else START_AT
                for slot in range(SLOTS):
                    if experts:
                        expert_slot(g, slot)
                    if wkv:
                        wkv_slot(g + 2, slot, at)
                    if layer:
                        layer_slot(g + 1, slot, at, wkv)

            pe.wait_ge(s["ident_ready"], 2)
            passage(-2, False, False, True)
            passage(-1, False, True, True)
            pe.wait_ge(s["gate_lo_ready"], 1)
            passage(0, True, True, True)
            with pe.Fori(1, NG - 2) as g:
                passage(g, True, True, True)
            passage(NG - 2, True, True, False)
            passage(NG - 1, True, False, False)

        @block.scalar
        def _(act):
            def expert_slot(g, slot):
                for e in range(NE):
                    if slot == expert_at("tanh_done", e):
                        if isinstance(g, int) and g == 0 and e < 2:
                            act.wait_ge(s["split_lo_done"], raw_out[f"act_buf {e}"])
                        act.wait_ge(s["h1_done"], NE * g + e + 1)
                        wait(act, s["glo_ready"], NE * g + e - 1)
                        nc.scalar.activation(act_buf[:, e % 2], bank_h1[e % 2][:], ACT.Tanh, scale=0.5).then_inc(s["tanh_done"], 1)
                    if slot == expert_at("ghi_ready", e):
                        if isinstance(g, int) and g == 0 and e < 2:
                            act.wait_ge(s["split_lo_done"], raw_out[f"gated_hi {e}"])
                        act.wait_ge(s["gated_ready"], NE * g + e + 1)
                        wait(act, s["out_done"], NE * g + e - 1)
                        nc.scalar.activation(flat(gated_hi[:, e % 2]), act_buf[:, e % 2], ACT.Copy).then_inc(s["ghi_ready"], 1)
                if slot == AT["logits_out"]:
                    act.wait_ge(s["logits_done"], g + 1)
                    wait(act, s["r_step"], ROUTER_STEPS * g)
                    nc.scalar.activation(logitsT, bank_out[0:NE, 0:N], ACT.Copy).then_inc(s["logits_out"], 1)
                if slot == AT["r_exp"]:
                    act.wait_ge(s["r_centred"], g + 1)
                    nc.scalar.activation(prb[:, 1], prb[:, 0], ACT.Exp).then_inc(s["r_exp"], 1)

            def split_hi(dst, src, done, scale=1.0):
                nc.scalar.activation(dst, src, ACT.Copy, scale=scale).then_inc(done, 1)

            def relu(f, p):
                if isinstance(f, int) and f == 0 and p == 0:
                    act.wait_ge(s["ld_upcol"], 16)
                act.wait_ge(s["up_done"], PAIRS * f + p + 1)
                if p == 0:
                    wait(act, s["ptr_done"], f)
                else:
                    wait(act, s["hid_lo_ready"], PAIRS * f + p - 1)
                for k in range(2):
                    last = nc.scalar.activation(hid[:, p % 2, k * N:(k + 1) * N], hidden_bank(f, p)[:, k * N:(k + 1) * N],
                                                ACT.Relu, scale=up_col[:, 2 * p + k:2 * p + k + 1])
                last.then_inc(s["hid_ready"], 1)

            def relu_hi(f, p):
                act.wait_ge(s["hid_ready"], PAIRS * f + p + 1)
                if p == 0:
                    wait(act, s["score_done"], f)
                elif p == 1:
                    wait(act, s["wo_done"], f)
                else:
                    wait(act, s["dn_done"], PAIRS * f + p - 1)
                split_hi(flat(hid_hi[:, p % 2]), hid[:, p % 2], s["hid_hi_ready"])

            def wkv_slot(g, slot, at):
                if slot == at["exp_done"]:
                    act.wait_ge(s["ktr_done"], g + 1)
                    if isinstance(g, int) and g == 0:
                        act.wait_ge(s["chan_step"], 7)
                    for dst, row in ((ea, 3), (eb, 4)):
                        for c in range(C):
                            last = nc.scalar.activation(flat(dst[:, c]), side[0][:, c * N:(c + 1) * N], ACT.Exp,
                                                        bias=chan[:, row, c:c + 1])
                    last.then_inc(s["exp_done"], 1)
                if slot == at["x1h_ready"]:
                    act.wait_ge(s["ltr1_done"], g + 1)
                    wait(act, s["pv_done"], g)
                    split_hi(flat(xh[:]), side[2][:], s["x1h_ready"])
                if slot == at["hid_ready"][0]:
                    relu(g, 0)
                if slot == at["hid_hi_ready"][0]:
                    relu_hi(g, 0)

            def layer_slot(f, slot, at):
                for p in range(1, PAIRS):
                    if slot == at["hid_ready"][p]:
                        relu(f, p)
                    if slot == at["hid_hi_ready"][p]:
                        relu_hi(f, p)
                if slot == at["x2h_ready"]:
                    act.wait_ge(s["ltr2_done"], f + 1)
                    split_hi(flat(xh[:]), side[0][:], s["x2h_ready"])
                if slot == at["qh_ready"]:
                    act.wait_ge(s["q_done"], f + 1)
                    split_hi(flat(qh), side[2][:], s["qh_ready"], scale=float(D) ** -0.5)
                if slot == at["kh_ready"]:
                    act.wait_ge(s["k_done"], f + 1)
                    split_hi(flat3(kh[:, 1]), side[1][:], s["kh_ready"])
                if slot == at["vh_ready"]:
                    act.wait_ge(s["v_done"], f + 1)
                    split_hi(flat(vh[:, 1]), side[0][:], s["vh_ready"])
                if slot == at["kc_hi"]:
                    act.wait_ge(s["ld_ctxT"], 16 * C * (f + 1))
                    wait(act, s["score_done"], f)
                    split_hi(flat3(kh[:, 0]), flat3(ctxT_a[:]), s["kc_hi"])
                if slot == at["vc_hi"]:
                    act.wait_ge(s["ld_ctx"], 16 * (f + 1))
                    wait(act, s["pv_done"], f)
                    split_hi(flat(vh[:, 0]), flat(ctx_a[:]), s["vc_hi"])
                if slot == at["exp_p_done"]:
                    act.wait_ge(s["negmax_ready"], f + 1)
                    for b in range(G):
                        last = nc.scalar.activation(prob[:, b].rearrange("p k t -> p (k t)"),
                                                    side[2][:, b * 2 * T:(b + 1) * 2 * T], ACT.Exp,
                                                    bias=row_max[:, 1, b:b + 1], accum_out=row_sum[:, b:b + 1])
                    last.then_inc(s["exp_p_done"], 1)
                if slot == at["pth_ready"]:
                    act.wait_ge(s["ptr_done"], f + 1)
                    split_hi(flat3(pth), side[1][:], s["pth_ready"])
                if slot == at["att_scaled"]:
                    act.wait_ge(s["pv_done"], f + 1)
                    act.wait_ge(s["rowinv_ready"], f + 1)
                    for b in range(G):
                        last = nc.scalar.activation(att[:, b], side[0][:, b * D:(b + 1) * D], ACT.Copy,
                                                    scale=row_inv[:, b:b + 1])
                    last.then_inc(s["att_scaled"], 1)
                if slot == at["oh_ready"]:
                    act.wait_ge(s["otr_done"], f + 1)
                    split_hi(flat(oh), side[2][:], s["oh_ready"])
                if slot == at["xmh_ready"]:
                    act.wait_ge(s["ltr3_done"], f + 1)
                    split_hi(flat(xmh[:]), side[0][:], s["xmh_ready"])

            def split_piece(n):
                act.wait_ge(landed[n % RING], 16 * (n // RING + 1))
                split_hi(splits[n - SIGNS][0], ring[n % RING], s["split_hi_done"])

            def passage(g, experts, layer, wkv):
                at = AT if experts else START_AT
                for slot in range(SLOTS):
                    if experts:
                        expert_slot(g, slot)
                    if wkv:
                        wkv_slot(g + 2, slot, at)
                    if layer:
                        layer_slot(g + 1, slot, at)
                    if not experts:
                        for n in pieces_of(HI_AT, layer, slot):
                            split_piece(SIGNS + n)

            act.wait_ge(s["chan_step"], 1)
            nc.scalar.activation(chan[:, 5], chan[:, 5], ACT.Exp).then_inc(s["chan_step"], 1)
            act.wait_ge(s["ld_gates"], 48)
            nc.scalar.activation(gates[:], gates_raw[:, 0:4], ACT.Tanh).then_inc(s["gates_ready"], 1)
            passage(-2, False, False, True)
            act.wait_ge(s["ld_gatew"], 16)
            split_hi(flat(gate_hi[:]), flat(gate_raw[:]), s["gate_hi_ready"])
            passage(-1, False, True, True)
            passage(0, True, True, True)
            with act.Fori(1, NG - 2) as g:
                passage(g, True, True, True)
            passage(NG - 2, True, True, False)
            passage(NG - 1, True, False, False)

        @block.gpsimd
        def _(pool):
            def add_eps(mv, rv, i, count):
                pool.wait_ge(s[f"mv{i}_done"], count)
                nc.gpsimd.tensor_tensor(rv[:, 0], mv[:, :, 1], eps[:], ALU.add).then_inc(s[f"var{i}_done"], 1)

            def rstd(rv, i, count):
                pool.wait_ge(s[f"var{i}_done"], count)
                nc.gpsimd.tensor_tensor(rv[:, 1], rv[:, 0], minus_half[:], ALU.pow).then_inc(s[f"rstd{i}_done"], 1)

            def expert_slot(g, slot):
                for e in range(NE):
                    if slot == expert_at("glo_ready", e):
                        if isinstance(g, int) and g == 0 and e < 2:
                            pool.wait_ge(s["split_lo_done"], raw_out[f"gated_lo {e}"])
                        pool.wait_ge(s["ghi_ready"], NE * g + e + 1)
                        nc.gpsimd.tensor_tensor(flat(gated_lo[:, e % 2]), act_buf[:, e % 2], flat(f32(gated_hi[:, e % 2])),
                                                ALU.subtract).then_inc(s["glo_ready"], 1)

            def relu_lo(f, p):
                pool.wait_ge(s["hid_hi_ready"], PAIRS * f + p + 1)
                nc.gpsimd.tensor_tensor(flat(hid_lo[:, p % 2]), hid[:, p % 2], flat(f32(hid_hi[:, p % 2])),
                                        ALU.subtract).then_inc(s["hid_lo_ready"], 1)

            def wkv_slot(g, slot, at):
                if slot == at["var0_done"]:
                    add_eps(mv_w, rstd_w, 0, g + 1)
                if slot == at["rstd0_done"]:
                    rstd(rstd_w, 0, g + 1)
                if slot == at["ramp_added"]:
                    pool.wait_ge(s["norm0_done"], g + 1)
                    for b in range(G):
                        last = nc.gpsimd.tensor_tensor(xwn[:, b], xwn[:, b], ramp[:], ALU.add)
                    last.then_inc(s["ramp_added"], 1)
                if slot == at["ebv_ready"]:
                    pool.wait_ge(s["den_ready"], g + 1)
                    nc.gpsimd.tensor_tensor(flat3(eb[:]), flat3(eb[:]), flat3(vT[:]), ALU.mult).then_inc(s["ebv_ready"], 1)
                if slot == at["num_ready"]:
                    pool.wait_ge(s["ebv_ready"], g + 1)
                    pool.wait_ge(s["p_scanned"], g + 1)
                    nc.gpsimd.tensor_tensor(p_late, p_late, flat3(eb[:]), ALU.add).then_inc(s["num_ready"], 1)
                if slot == at["var1_done"]:
                    add_eps(mv_1, rstd_1, 1, g + 1)
                if slot == at["rstd1_done"]:
                    rstd(rstd_1, 1, g + 1)
                if slot == at["hid_lo_ready"][0]:
                    relu_lo(g, 0)

            def layer_slot(f, slot, at):
                for p in range(1, PAIRS):
                    if slot == at["hid_lo_ready"][p]:
                        relu_lo(f, p)
                for i in (2, 3):
                    if slot == at[f"var{i}_done"]:
                        add_eps(mv_f, rstd_f, i, f + 1)
                    if slot == at[f"rstd{i}_done"]:
                        rstd(rstd_f, i, f + 1)
                if slot == at["kc_lo"]:
                    pool.wait_ge(s["kc_hi"], f + 1)
                    nc.gpsimd.tensor_tensor(flat3(kl[:, 0]), flat3(ctxT_a[:]), flat3(f32(kh[:, 0])),
                                            ALU.subtract).then_inc(s["kc_lo"], 1)
                if slot == at["vc_lo"]:
                    pool.wait_ge(s["vc_hi"], f + 1)
                    nc.gpsimd.tensor_tensor(flat(vl[:, 0]), flat(ctx_a[:]), flat(f32(vh[:, 0])),
                                            ALU.subtract).then_inc(s["vc_lo"], 1)

            def split_piece(n):
                hi, lo = splits[n - SIGNS]
                pool.wait_ge(s["split_hi_done"], n - SIGNS + 1)
                nc.gpsimd.tensor_tensor(lo, ring[n % RING], f32(hi),
                                        ALU.subtract).then_inc(s["split_lo_done"], 1)

            def passage(g, experts, layer, wkv):
                at = AT if experts else START_AT
                for slot in range(SLOTS):
                    if experts:
                        expert_slot(g, slot)
                    if wkv:
                        wkv_slot(g + 2, slot, at)
                    if layer:
                        layer_slot(g + 1, slot, at)
                    if not experts:
                        for n in pieces_of(LO_AT, layer, slot):
                            split_piece(SIGNS + n)

            nc.gpsimd.memset(minus_half[:], -0.5).then_inc(s["consts_pool"], 1)
            nc.gpsimd.memset(eps[:], EPS).then_inc(s["consts_pool"], 1)
            nc.gpsimd.iota(time_col[:], pattern=[[0, 1]], base=0, channel_multiplier=-1,
                           allow_small_or_imprecise_dtypes=True).then_inc(s["consts_pool"], 1)
            nc.gpsimd.memset(ident[:], 0.0).then_inc(s["ident_ready"], 1)
            pool.wait_ge(s["ident_ready"], 1)
            nc.gpsimd.affine_select(out=ident[:], in_=ident[:], compare_op=ALU.not_equal, fill=1.0, base=0,
                                    pattern=[[-1, P]], channel_multiplier=1).then_inc(s["ident_ready"], 1)
            nc.gpsimd.memset(router_bias[:], NEVER).then_inc(s["bias_fill"], 1)
            nc.gpsimd.memset(gate_raw[:], 0.0).then_inc(s["bias_fill"], 1)
            nc.gpsimd.memset(earlier[:], 0.0).then_inc(s["consts_pool"], 1)
            pool.wait_ge(s["consts_pool"], 4)
            for e in range(1, NE):
                last = nc.gpsimd.memset(earlier[:, e, 0:e], 1.0)
            last.then_inc(s["consts_pool"], 1)
            pool.wait_ge(s["ramp_ready"], 1)
            passage(-2, False, False, True)
            pool.wait_ge(s["gate_hi_ready"], 1)
            nc.gpsimd.tensor_tensor(flat(gate_lo[:]), flat(gate_raw[:]), flat(f32(gate_hi[:])),
                                    ALU.subtract).then_inc(s["gate_lo_ready"], 1)
            passage(-1, False, True, True)
            passage(0, True, True, True)
            with pool.Fori(1, NG - 2) as g:
                passage(g, True, True, True)
            passage(NG - 2, True, True, False)
            passage(NG - 1, True, False, False)

        @block.vector
        def _(dve):
            def stats(src, stat, i):
                for b in range(G):
                    last = nc.vector.bn_stats(stat[:, b], src[:, b])
                last.then_inc(s[f"stat{i}_done"], 1)

            def mean_var(stat, mv, i, count):
                dve.wait_ge(s[f"stat{i}_done"], count)
                nc.vector.memset(scratch[:], 0.0)
                for b in range(G):
                    last = nc.vector.bn_aggr(mv[:, b], stat[:, b])
                last.then_inc(s[f"mv{i}_done"], 1)

            def normalise(dst, src, mv, rv, i):
                for b in range(G):
                    last = nc.vector.tensor_scalar(dst[:, b], src[:, b], mv[:, b, 0:1], rv[:, 1, b:b + 1],
                                                   ALU.subtract, ALU.mult)
                last.then_inc(s[f"norm{i}_done"], 1)

            def split_lo(dst, src, hi, done):
                nc.vector.tensor_tensor(dst, src, hi, ALU.subtract).then_inc(done, 1)

            def router(g, slot):
                base = ROUTER_STEPS * g

                def due(k):
                    if slot == AT["r_step"][k - 1] and k > 1:
                        dve.wait_ge(s["r_step"], base + k - 1)
                    return slot == AT["r_step"][k - 1]

                logits, expo, probs, biased, rank, chosen = (prb[:, i] for i in range(6))

                def by_expert(col):
                    return col.unsqueeze(2).to_broadcast([P, G, NE])

                def bias(i):
                    return router_bias[:, i].unsqueeze(1).to_broadcast([P, G, NE])

                if due(1):
                    dve.wait_ge(s["logits_turned"], g + 1)
                    nc.vector.tensor_tensor(logits, bank_out[:, 0:G * NE].rearrange("p (b e) -> p b e", b=G),
                                            bias(0), ALU.add).then_inc(s["r_step"], 1)
                if due(2):
                    nc.vector.reduce_max(red[:, 0], logits, AX_X).then_inc(s["r_step"], 1)
                if slot == AT["r_centred"]:
                    dve.wait_ge(s["r_step"], base + 2)
                    nc.vector.tensor_tensor(logits, logits, by_expert(red[:, 0]), ALU.subtract).then_inc(s["r_centred"], 1)
                if due(3):
                    dve.wait_ge(s["r_exp"], g + 1)
                    nc.vector.reduce_sum(red[:, 1], expo, AX_X).then_inc(s["r_step"], 1)
                if due(4):
                    nc.vector.reciprocal(red[:, 2], red[:, 1]).then_inc(s["r_step"], 1)
                if due(5):
                    nc.vector.tensor_tensor(probs, expo, by_expert(red[:, 2]), ALU.mult).then_inc(s["r_step"], 1)
                if due(6):
                    nc.vector.tensor_tensor(biased, probs, bias(1), ALU.add).then_inc(s["r_step"], 1)
                other = biased.unsqueeze(2).to_broadcast([P, G, NE, NE])
                own = biased.unsqueeze(3).to_broadcast([P, G, NE, NE])
                if due(7):
                    nc.vector.tensor_tensor(cmp_gt, other, own, ALU.is_gt).then_inc(s["r_step"], 1)
                if due(8):
                    nc.vector.tensor_tensor(cmp_eq, other, own, ALU.is_equal).then_inc(s["r_step"], 1)
                if due(9):
                    nc.vector.tensor_tensor(cmp_eq, cmp_eq, earlier[:].unsqueeze(1).to_broadcast([P, G, NE, NE]),
                                            ALU.mult).then_inc(s["r_step"], 1)
                if due(10):
                    nc.vector.tensor_tensor(cmp_gt, cmp_gt, cmp_eq, ALU.add).then_inc(s["r_step"], 1)
                if due(11):
                    nc.vector.reduce_sum(rank, cmp_gt, AX_X).then_inc(s["r_step"], 1)
                if due(12):
                    nc.vector.scalar_tensor_tensor(chosen, rank, float(TOP_K), probs, ALU.is_lt, ALU.mult).then_inc(s["r_step"], 1)
                if due(13):
                    nc.vector.reduce_sum(red[:, 3], chosen, AX_X).then_inc(s["r_step"], 1)
                if due(14):
                    nc.vector.reciprocal(red[:, 4], red[:, 3]).then_inc(s["r_step"], 1)
                if due(15):
                    nc.vector.tensor_scalar(red[:, 4], red[:, 4], half_gate[:], None, ALU.mult).then_inc(s["r_step"], 1)
                if due(16):
                    nc.vector.tensor_tensor(wgt[:], chosen, by_expert(red[:, 4]), ALU.mult).then_inc(s["r_step"], 1)
                if slot == AT["wgt_ready"]:
                    dve.wait_ge(s["r_step"], base + ROUTER_STEPS)
                    nc.vector.tensor_copy(wgt[:, :, NE - 1], half_gate[:].to_broadcast([P, G])).then_inc(s["wgt_ready"], 1)

            def expert_slot(g, slot):
                for e in range(NE):
                    if slot == ACC_AT[e]:
                        dve.wait_ge(s["out_done"], NE * g + e + 1)
                        if e == 0:
                            if isinstance(g, int) and g == 0:
                                dve.wait_ge(s["split_lo_done"], raw_out["acc"])
                            dve.wait_ge(s["wgt_ready"], g + 1)
                            wait(dve, s["stored"], 16 * g)
                        else:
                            dve.wait_ge(s["acc_done"], NE * g + e)
                        for b in range(G):
                            last = nc.vector.scalar_tensor_tensor(acc[:, b], bank_out[:, b * D:(b + 1) * D], wgt[:, b, e:e + 1],
                                                                  (x23 if e == 0 else acc)[:, b], ALU.mult, ALU.add)
                        last.then_inc(s["acc_done"], 1)
                    if slot == expert_at("act_done", e):
                        dve.wait_ge(s["tanh_done"], NE * g + e + 1)
                        nc.vector.scalar_tensor_tensor(act_buf[:, e % 2], act_buf[:, e % 2], 1.0, bank_h1[e % 2][:],
                                                       ALU.add, ALU.mult).then_inc(s["act_done"], 1)
                    if slot == expert_at("gated_ready", e):
                        dve.wait_ge(s["h2_done"], NE * g + e + 1)
                        dve.wait_ge(s["act_done"], NE * g + e + 1)
                        nc.vector.tensor_tensor(act_buf[:, e % 2], act_buf[:, e % 2], bank_h2[e % 2][:],
                                                ALU.mult).then_inc(s["gated_ready"], 1)
                router(g, slot)

            def wkv_slot(g, slot, at):
                if slot == at["stat0_done"]:
                    dve.wait_ge(s["ld_x"], 16 * (g + 1))
                    stats(xw, stat_w, 0)
                if slot == at["mv0_done"]:
                    mean_var(stat_w, mv_w, 0, g + 1)
                if slot == at["norm0_done"]:
                    dve.wait_ge(s["rstd0_done"], g + 1)
                    normalise(xwn, xw, mv_w, rstd_w, 0)
                if slot == at["q_scanned"]:
                    dve.wait_ge(s["exp_done"], g + 1)
                    nc.vector.tensor_tensor_scan(q_state[:, 1:], flat3(decay[:]), flat3(ea[:]), 0.0, ALU.mult,
                                                 ALU.add).then_inc(s["q_scanned"], 1)
                if slot == at["den_ready"]:
                    dve.wait_ge(s["q_scanned"], g + 1)
                    nc.vector.tensor_tensor(q_late, q_late, flat3(eb[:]), ALU.add).then_inc(s["den_ready"], 1)
                if slot == at["eav_ready"]:
                    dve.wait_ge(s["ld_v"], 16 * C * (g + 1))
                    dve.wait_ge(s["q_scanned"], g + 1)
                    nc.vector.tensor_tensor(flat3(ea[:]), flat3(ea[:]), flat3(vT[:]), ALU.mult).then_inc(s["eav_ready"], 1)
                if slot == at["p_scanned"]:
                    dve.wait_ge(s["eav_ready"], g + 1)
                    nc.vector.tensor_tensor_scan(p_state[:, 1:], flat3(decay[:]), flat3(ea[:]), 0.0, ALU.mult,
                                                 ALU.add).then_inc(s["p_scanned"], 1)
                parts = len(at["den_inv"])
                for i in range(parts):
                    if slot == at["den_inv"][i]:
                        dve.wait_ge(s["den_ready"], g + 1)
                        part = q_state[:, i * C * N // parts:(i + 1) * C * N // parts]
                        nc.vector.reciprocal(part, part).then_inc(s["den_inv"], 1)
                if slot == at["y_raw"]:
                    dve.wait_ge(s["num_ready"], g + 1)
                    dve.wait_ge(s["den_inv"], parts * (g + 1))
                    nc.vector.tensor_tensor(flat3(ea[:]), p_late, q_late, ALU.mult).then_inc(s["y_raw"], 1)
                if slot == at["y_ready"]:
                    dve.wait_ge(s["y_raw"], g + 1)
                    nc.vector.tensor_copy(ea[:, :, :, 0], vT[:, :, :, 0]).then_inc(s["y_ready"], 1)
                if slot == at["x1_ready"]:
                    dve.wait_ge(s["ytr_done"], g + 1)
                    wait(dve, s["x2_ready"], g)
                    nc.vector.scalar_tensor_tensor(flat(x1[:]), side[1][:], gates[:, 0:1], flat(xw[:]), ALU.mult,
                                                   ALU.add).then_inc(s["x1_ready"], 1)
                if slot == at["stat1_done"]:
                    dve.wait_ge(s["x1_ready"], g + 1)
                    stats(x1, stat_1, 1)
                if slot == at["mv1_done"]:
                    mean_var(stat_1, mv_1, 1, g + 1)
                if slot == at["norm1_done"]:
                    dve.wait_ge(s["rstd1_done"], g + 1)
                    normalise(x1n, x1, mv_1, rstd_1, 1)
                if slot == at["x1l_ready"]:
                    dve.wait_ge(s["x1h_ready"], g + 1)
                    split_lo(flat(xl[:]), side[2][:], flat(f32(xh[:])), s["x1l_ready"])

            def layer_slot(f, slot, at):
                if slot == at["ffn_scaled"]:
                    dve.wait_ge(s["dn_done"], PAIRS * f + PAIRS)
                    wait(dve, s["acc_done"], NE * f - NE + 1)
                    nc.vector.tensor_tensor(x23[:], side[1][:].rearrange("p (b d) -> p b d", b=G),
                                            down_row[:].unsqueeze(1).to_broadcast([P, G, D]), ALU.mult).then_inc(s["ffn_scaled"], 1)
                if slot == at["x2_ready"]:
                    dve.wait_ge(s["ffn_scaled"], f + 1)
                    nc.vector.tensor_tensor(x23[:], x23[:], x1[:], ALU.add).then_inc(s["x2_ready"], 1)
                if slot == at["stat2_done"]:
                    dve.wait_ge(s["x2_ready"], f + 1)
                    stats(x23, stat_f, 2)
                if slot == at["mv2_done"]:
                    mean_var(stat_f, mv_f, 2, f + 1)
                if slot == at["norm2_done"]:
                    dve.wait_ge(s["rstd2_done"], f + 1)
                    normalise(xfn, x23, mv_f, rstd_f, 2)
                if slot == at["x2l_ready"]:
                    dve.wait_ge(s["x2h_ready"], f + 1)
                    split_lo(flat(xl[:]), side[0][:], flat(f32(xh[:])), s["x2l_ready"])
                if slot == at["ql_ready"]:
                    dve.wait_ge(s["qh_ready"], f + 1)
                    nc.vector.scalar_tensor_tensor(flat(ql), side[2][:], float(D) ** -0.5, flat(f32(qh)), ALU.mult,
                                                   ALU.subtract).then_inc(s["ql_ready"], 1)
                if slot == at["kl_ready"]:
                    dve.wait_ge(s["kh_ready"], f + 1)
                    split_lo(flat3(kl[:, 1]), side[1][:], flat3(f32(kh[:, 1])), s["kl_ready"])
                if slot == at["vl_ready"]:
                    dve.wait_ge(s["vh_ready"], f + 1)
                    split_lo(flat(vl[:, 1]), side[0][:], flat(f32(vh[:, 1])), s["vl_ready"])
                if slot == at["max_ready"]:
                    dve.wait_ge(s["score_done"], f + 1)
                    nc.vector.reduce_max(row_max[:, 0], side[2][:].rearrange("p (b k) -> p b k", b=G), AX_X).then_inc(s["max_ready"], 1)
                if slot == at["negmax_ready"]:
                    dve.wait_ge(s["max_ready"], f + 1)
                    nc.vector.tensor_scalar(row_max[:, 1], row_max[:, 0], -1.0, None, ALU.mult).then_inc(s["negmax_ready"], 1)
                if slot == at["rowinv_ready"]:
                    dve.wait_ge(s["exp_p_done"], f + 1)
                    nc.vector.reciprocal(row_inv[:], row_sum[:]).then_inc(s["rowinv_ready"], 1)
                if slot == at["ptl_ready"]:
                    dve.wait_ge(s["pth_ready"], f + 1)
                    split_lo(flat3(ptl), side[1][:], flat3(f32(pth)), s["ptl_ready"])
                if slot == at["ol_ready"]:
                    dve.wait_ge(s["oh_ready"], f + 1)
                    split_lo(flat(ol), side[2][:], flat(f32(oh)), s["ol_ready"])
                if slot == at["x3_ready"]:
                    dve.wait_ge(s["wo_done"], f + 1)
                    nc.vector.scalar_tensor_tensor(flat(x23[:]), side[1][:], gates[:, 1:2], flat(x23[:]), ALU.mult,
                                                   ALU.add).then_inc(s["x3_ready"], 1)
                if slot == at["stat3_done"]:
                    dve.wait_ge(s["x3_ready"], f + 1)
                    stats(x23, stat_f, 3)
                if slot == at["mv3_done"]:
                    mean_var(stat_f, mv_f, 3, f + 1)
                if slot == at["norm3_done"]:
                    dve.wait_ge(s["rstd3_done"], f + 1)
                    normalise(xfn, x23, mv_f, rstd_f, 3)
                if slot == at["xml_ready"]:
                    dve.wait_ge(s["xmh_ready"], f + 1)
                    split_lo(flat(xml[:]), side[0][:], flat(f32(xmh[:])), s["xml_ready"])

            below_zero = (xmh[:], xml[:])

            def sign_piece(n):
                dve.wait_ge(landed[n % RING], 16 * (n // RING + 1))
                raw = ring[n % RING]
                negative = below_zero[n % 2]
                wait(dve, s["sign_done"], n - 1)
                nc.vector.tensor_scalar(negative, raw, 0.0, None, ALU.is_lt).then_inc(s["sign_neg"], 1)
                dve.wait_ge(s["sign_neg"], n + 1)
                nc.vector.scalar_tensor_tensor(signs[n], raw, 0.0, f32(negative), ALU.is_gt, ALU.subtract).then_inc(s["sign_done"], 1)

            def scan_constants():
                nc.vector.memset(decay[:], 1.0).then_inc(s["decay_step"], 1)
                dve.wait_ge(s["decay_step"], 1)
                for c in range(C):
                    last = nc.vector.tensor_scalar(flat(decay[:, c]), flat(decay[:, c]), chan[:, 5, c:c + 1], None, ALU.mult)
                last.then_inc(s["decay_step"], 1)
                dve.wait_ge(s["decay_step"], 2)
                nc.vector.memset(decay[:, :, :, 0], 0.0).then_inc(s["decay_step"], 1)
                nc.vector.memset(q_state[:, 0:1], 1.0).then_inc(s["decay_step"], 1)
                dve.wait_ge(s["decay_step"], 4)
                dve.wait_ge(s["gates_ready"], 1)
                nc.vector.tensor_scalar(half_gate[:], gates[:, 3:4], 0.5, None, ALU.mult).then_inc(s["scales_ready"], 1)
                dve.wait_ge(s["ld_drow"], 16)
                nc.vector.tensor_scalar(down_row[:], down_row[:], gates_raw[:, 4:5], gates[:, 2:3], ALU.mult,
                                        ALU.mult).then_inc(s["scales_ready"], 1)
                dve.wait_ge(s["scales_ready"], 2)

            def passage(g, experts, layer, wkv):
                at = AT if experts else START_AT
                for slot in range(SLOTS):
                    if not layer and not experts and slot == SCAN_CONSTANTS_AT:
                        scan_constants()
                    if experts:
                        expert_slot(g, slot)
                    if wkv:
                        wkv_slot(g + 2, slot, at)
                    if layer:
                        layer_slot(g + 1, slot, at)
                    if not experts:
                        for n in pieces_of(SIGN_AT, layer, slot):
                            sign_piece(n)

            w_col, u_col = wu[:, 0], wu[:, 1]
            dve.wait_ge(s["ld_wu"], 32)
            nc.vector.tensor_scalar(chan[:, 5], w_col, 0.0, None, ALU.min).then_inc(s["chan_step"], 1)
            dve.wait_ge(s["chan_step"], 2)
            nc.vector.tensor_scalar(chan[:, 0], w_col, 0.0, None, ALU.max).then_inc(s["chan_step"], 1)
            dve.wait_ge(s["chan_step"], 3)
            nc.vector.tensor_scalar(chan[:, 1], chan[:, 0], -1.0, None, ALU.mult).then_inc(s["chan_step"], 1)
            dve.wait_ge(s["chan_step"], 4)
            nc.vector.tensor_tensor(chan[:, 2], chan[:, 1], u_col, ALU.max).then_inc(s["chan_step"], 1)
            dve.wait_ge(s["chan_step"], 5)
            nc.vector.tensor_tensor(chan[:, 3], chan[:, 1], chan[:, 2], ALU.subtract).then_inc(s["chan_step"], 1)
            nc.vector.tensor_tensor(chan[:, 4], u_col, chan[:, 2], ALU.subtract).then_inc(s["chan_step"], 1)
            dve.wait_ge(s["ld_ramp"], 16)
            dve.wait_ge(s["consts_pool"], 5)
            nc.vector.tensor_scalar(ramp[:], ramp[:], 0.0, time_col[:], ALU.max, ALU.mult).then_inc(s["ramp_ready"], 1)
            passage(-2, False, False, True)
            dve.wait_ge(s["ld_rbias"], 32)
            passage(-1, False, True, True)
            passage(0, True, True, True)
            with dve.Fori(1, NG - 2) as g:
                passage(g, True, True, True)
            passage(NG - 2, True, True, False)
            passage(NG - 1, True, False, False)


def kernel(**inputs):
    import numpy as _np
    import concourse.bacc as _bacc
    from concourse import mybir as _mybir
    from concourse.bass_utils import run_bass_kernel_spmd as _run

    layout = [
        ("x", inputs["x"]),
        ("ctx_in", inputs["ctx_2048"]),
        ("ctxT_in", _np.transpose(inputs["ctx_2048"], (0, 2, 1))),
        ("g_xattn", inputs["g_xattn"]), ("g_ffn", inputs["g_ffn"]),
        ("w_in", inputs["L0_xattn_w"]),
        ("w_cols", _np.transpose(inputs["L0_xattn_w"].reshape(-1, P))),
        ("u_cols", _np.transpose(inputs["L0_xattn_u"].reshape(-1, P))),
        ("upT_in", _np.transpose(inputs["L0_ffn_up_weight"])),
        ("downT_in", _np.transpose(inputs["L0_ffn_down_weight"])),
        ("up_cols", _np.transpose(inputs["L0_ffn_up_scale"].reshape(-1, P))),
         ("down_scale", inputs["L0_ffn_down_scale"]),
        ("output_scale", inputs["L0_ffn_output_scale"]),
        ("wqT_in", _np.transpose(inputs["L1_xattn_wq"])), ("wkT_in", _np.transpose(inputs["L1_xattn_wk"])),
        ("wvT_in", _np.transpose(inputs["L1_xattn_wv"])), ("woT_in", _np.transpose(inputs["L1_xattn_wo"])),
        ("W1", inputs["L1_ffn_W1"]), ("Wg", inputs["L1_ffn_Wg"]), ("W2", inputs["L1_ffn_W2"]),
        ("Ws1", inputs["L1_ffn_Ws1"]), ("Wsg", inputs["L1_ffn_Wsg"]), ("Ws2", inputs["L1_ffn_Ws2"]),
        ("gate_w", inputs["L1_ffn_gate_w"]), ("gate_b", inputs["L1_ffn_gate_b"]), ("biases", inputs["L1_ffn_biases"]),
    ]
    nc = _bacc.Bacc("TRN2", target_bir_lowering=False, num_devices=1)
    arrays, args = {}, {}
    for name, a in layout:
        a = _np.ascontiguousarray(a)
        arrays[f"in_{name}"] = a
        args[name] = nc.dram_tensor(f"in_{name}", a.shape, _mybir.dt.from_np(a.dtype), kind="ExternalInput").ap()
    args["out"] = nc.dram_tensor("out_0", inputs["x"].shape, _mybir.dt.float32, kind="ExternalOutput").ap()
    flamingo_kernel(nc, **args)
    return _run(nc, [arrays], core_ids=[0]).results[0]["out_0"]
```
